# Optimizing a Trainium2 kernel written in Bass

```python
import numpy as np
import jax
import jax.numpy as jnp

def _softmax(x, axis=-1):
    return jax.nn.softmax(x, axis=axis)

def _gelu(x):
    return jax.nn.gelu(x, approximate=True)

def _silu(x):
    return jax.nn.silu(x)

def _sigmoid(x):
    return jax.nn.sigmoid(x)

def _layernorm(x, axis=-1, eps=1e-05):
    m = jnp.mean(x, axis=axis, keepdims=True)
    v = jnp.var(x, axis=axis, keepdims=True)
    return (x - m) / jnp.sqrt(v + eps)

def _scatter_add(tgt, idx, src, axis=0):
    return tgt.at[idx].add(src)

def _segment_sum(src, seg, n):
    return jax.ops.segment_sum(src, seg, n)
kernel_name = 'mk_flamingo_gated_d1_seqx_r4_268c7f'

def setup_inputs(seed: int=0):
    np.random.seed(seed)
    _w = jnp.asarray

    def _rec_inputs():
        import jax
        import jax.numpy as jnp
        _rk = jax.random.key(seed)
        x = -0.000125 + 0.9999 * jax.random.normal(jax.random.fold_in(_rk, 1), (32, 128, 512), jnp.float32)
        _lenS = 128 - jax.random.randint(jax.random.fold_in(_rk, 7), (32,), 0, max(1, 128 // 4) + 1, jnp.int32)
        _lenS2 = 128 - jax.random.randint(jax.random.fold_in(_rk, 8), (32,), 0, max(1, 128 // 4) + 1, jnp.int32)
        _ctx_2048P = jax.random.normal(jax.random.fold_in(_rk, 11), (32, 16, 512), jnp.float32)
        _ctx_2048c = jax.random.dirichlet(jax.random.fold_in(_rk, 511), 0.3 * jnp.ones((16,), jnp.float32), (32, 128))
        _ctx_2048t = jnp.einsum('bsk,bkd->bsd', _ctx_2048c, _ctx_2048P)
        _ctx_2048t = _ctx_2048t * jax.lax.rsqrt(jnp.mean(jnp.square(_ctx_2048t)) + 1e-12) * 0.953939
        ctx_2048 = 1.72703e-05 + 1.00003 * (_ctx_2048t + 0.3 * jax.random.normal(jax.random.fold_in(_rk, 611), (32, 128, 512), jnp.float32))
        _g = jax.random.normal(jax.random.fold_in(_rk, 9001), (2, 1), jnp.float32)
        _g = jnp.sign(_g) * jnp.maximum(jnp.abs(_g), 1.0) + (_g == 0) * 1.0
        g_xattn = _g[0]
        g_ffn = _g[1]
        return (x, ctx_2048, g_xattn, g_ffn)
    x, ctx_2048, g_xattn, g_ffn = _rec_inputs()

    def _L0_xattn_setup():
        import jax, jax.numpy as jnp
        import numpy as np
        DIM = 512
        NH = 16
        HD = DIM // NH
        EPS = 1e-06
        IMG_LEN = 257

        def rms_norm(x, w, eps=EPS):
            xf = x.astype(jnp.float32)
            y = xf * jax.lax.rsqrt(jnp.mean(xf * xf, axis=-1, keepdims=True) + eps)
            return y.astype(x.dtype) * w

        def linear(x, w, b):
            return jnp.einsum('blc,oc->blo', x, w) + b

        def attention(q, k, v):
            scale = 1.0 / jnp.sqrt(jnp.asarray(HD, q.dtype))
            scores = jnp.einsum('bqhd,bkhd->bhqk', q, k) * scale
            probs = jax.nn.softmax(scores, axis=-1)
            return jnp.einsum('bhqk,bkhd->bqhd', probs, v)
        key = jax.random.key(seed)
        ks = jax.random.split(key, 12)
        B, L = (2, 2048)
        s = 0.02
        inp = {'x': jax.random.normal(ks[0], (B, L, DIM), jnp.float32), 'context': jax.random.normal(ks[1], (B, 769, DIM), jnp.float32), 'q_w': jax.random.normal(ks[2], (DIM, DIM), jnp.float32) * s, 'q_b': jnp.zeros((DIM,), jnp.float32), 'k_w': jax.random.normal(ks[3], (DIM, DIM), jnp.float32) * s, 'k_b': jnp.zeros((DIM,), jnp.float32), 'v_w': jax.random.normal(ks[4], (DIM, DIM), jnp.float32) * s, 'v_b': jnp.zeros((DIM,), jnp.float32), 'k_img_w': jax.random.normal(ks[5], (DIM, DIM), jnp.float32) * s, 'k_img_b': jnp.zeros((DIM,), jnp.float32), 'v_img_w': jax.random.normal(ks[6], (DIM, DIM), jnp.float32) * s, 'v_img_b': jnp.zeros((DIM,), jnp.float32), 'o_w': jax.random.normal(ks[7], (DIM, DIM), jnp.float32) * s, 'o_b': jnp.zeros((DIM,), jnp.float32), 'norm_q_w': jnp.ones((DIM,), jnp.float32), 'norm_k_w': jnp.ones((DIM,), jnp.float32), 'norm_k_img_w': jnp.ones((DIM,), jnp.float32)}
        return inp
    _L0_xattn_all = _L0_xattn_setup()
    _L0_xattn_in = {k: v for k, v in _L0_xattn_all.items() if k in ('q_w', 'q_b', 'k_w', 'k_b', 'v_w', 'v_b', 'k_img_w', 'k_img_b', 'v_img_w', 'v_img_b', 'o_w', 'o_b', 'norm_q_w', 'norm_k_w', 'norm_k_img_w')}
    del _L0_xattn_all

    def _L0_ffn_setup():
        import jax, jax.numpy as jnp
        import numpy as np
        HID = 512
        INTER = 2048
        NEXP = 8
        TOPK = 2
        EPS = 1e-05

        def _mock_fused_moe(x, selected_experts, routing_weights, expert_weight):
            y = jnp.einsum('bsh,hd->bsd', x, expert_weight)
            scale = routing_weights.sum(axis=-1, keepdims=True)
            return y * scale
        key = jax.random.key(seed)
        ks = jax.random.split(key, 6)
        s = lambda fan_in: 1.0 / np.sqrt(fan_in)
        return {'hidden_states': jax.random.normal(ks[0], (4, 1024, HID), dtype=jnp.float32), 'gate_w': jax.random.uniform(ks[1], (HID, NEXP), jnp.float32, -s(HID), s(HID)), 'up_w': jax.random.uniform(ks[2], (HID, INTER), jnp.float32, -s(HID), s(HID)), 'down_w': jax.random.uniform(ks[3], (INTER, HID), jnp.float32, -s(INTER), s(INTER)), 'expert_weight': jax.random.normal(ks[4], (HID, HID), dtype=jnp.float32), 'ln_gamma': jnp.ones((HID,), jnp.float32), 'ln_beta': jnp.zeros((HID,), jnp.float32)}
    _L0_ffn_all = _L0_ffn_setup()
    _L0_ffn_in = {k: v for k, v in _L0_ffn_all.items() if k in ('gate_w', 'up_w', 'down_w', 'expert_weight', 'ln_gamma', 'ln_beta')}
    del _L0_ffn_all
    return {'x': x, 'ctx_2048': ctx_2048, 'g_xattn': g_xattn, 'g_ffn': g_ffn, 'L0_xattn_q_w': _L0_xattn_in['q_w'], 'L0_xattn_q_b': _L0_xattn_in['q_b'], 'L0_xattn_k_w': _L0_xattn_in['k_w'], 'L0_xattn_k_b': _L0_xattn_in['k_b'], 'L0_xattn_v_w': _L0_xattn_in['v_w'], 'L0_xattn_v_b': _L0_xattn_in['v_b'], 'L0_xattn_k_img_w': _L0_xattn_in['k_img_w'], 'L0_xattn_k_img_b': _L0_xattn_in['k_img_b'], 'L0_xattn_v_img_w': _L0_xattn_in['v_img_w'], 'L0_xattn_v_img_b': _L0_xattn_in['v_img_b'], 'L0_xattn_o_w': _L0_xattn_in['o_w'], 'L0_xattn_o_b': _L0_xattn_in['o_b'], 'L0_xattn_norm_q_w': _L0_xattn_in['norm_q_w'], 'L0_xattn_norm_k_w': _L0_xattn_in['norm_k_w'], 'L0_xattn_norm_k_img_w': _L0_xattn_in['norm_k_img_w'], 'L0_ffn_gate_w': _L0_ffn_in['gate_w'], 'L0_ffn_up_w': _L0_ffn_in['up_w'], 'L0_ffn_down_w': _L0_ffn_in['down_w'], 'L0_ffn_expert_weight': _L0_ffn_in['expert_weight'], 'L0_ffn_ln_gamma': _L0_ffn_in['ln_gamma'], 'L0_ffn_ln_beta': _L0_ffn_in['ln_beta']}

def reference(x, ctx_2048, g_xattn, g_ffn, L0_xattn_q_w, L0_xattn_q_b, L0_xattn_k_w, L0_xattn_k_b, L0_xattn_v_w, L0_xattn_v_b, L0_xattn_k_img_w, L0_xattn_k_img_b, L0_xattn_v_img_w, L0_xattn_v_img_b, L0_xattn_o_w, L0_xattn_o_b, L0_xattn_norm_q_w, L0_xattn_norm_k_w, L0_xattn_norm_k_img_w, L0_ffn_gate_w, L0_ffn_up_w, L0_ffn_down_w, L0_ffn_expert_weight, L0_ffn_ln_gamma, L0_ffn_ln_beta):
    import jax
    import jax.numpy as jnp

    def _L0_xattn_ref(x, context, q_w, q_b, k_w, k_b, v_w, v_b, k_img_w, k_img_b, v_img_w, v_img_b, o_w, o_b, norm_q_w, norm_k_w, norm_k_img_w):
        import jax, jax.numpy as jnp
        import numpy as np
        DIM = 512
        NH = 16
        HD = DIM // NH
        EPS = 1e-06
        IMG_LEN = 257

        def rms_norm(x, w, eps=EPS):
            xf = x.astype(jnp.float32)
            y = xf * jax.lax.rsqrt(jnp.mean(xf * xf, axis=-1, keepdims=True) + eps)
            return y.astype(x.dtype) * w

        def linear(x, w, b):
            return jnp.einsum('blc,oc->blo', x, w) + b

        def attention(q, k, v):
            scale = 1.0 / jnp.sqrt(jnp.asarray(HD, q.dtype))
            scores = jnp.einsum('bqhd,bkhd->bhqk', q, k) * scale
            probs = jax.nn.softmax(scores, axis=-1)
            return jnp.einsum('bhqk,bkhd->bqhd', probs, v)
        B, L, _ = x.shape
        ctx_img = context[:, :IMG_LEN]
        ctx_txt = context[:, IMG_LEN:]
        q = rms_norm(linear(x, q_w, q_b), norm_q_w).reshape(B, L, NH, HD)
        k = rms_norm(linear(ctx_txt, k_w, k_b), norm_k_w).reshape(B, -1, NH, HD)
        v = linear(ctx_txt, v_w, v_b).reshape(B, -1, NH, HD)
        k_img = rms_norm(linear(ctx_img, k_img_w, k_img_b), norm_k_img_w).reshape(B, -1, NH, HD)
        v_img = linear(ctx_img, v_img_w, v_img_b).reshape(B, -1, NH, HD)
        img_x = attention(q, k_img, v_img)
        txt_x = attention(q, k, v)
        out = (txt_x + img_x).reshape(B, L, DIM)
        return linear(out, o_w, o_b)

    def _L0_ffn_ref(hidden_states, gate_w, up_w, down_w, expert_weight, ln_gamma, ln_beta):
        import jax, jax.numpy as jnp
        import numpy as np
        HID = 512
        INTER = 2048
        NEXP = 8
        TOPK = 2
        EPS = 1e-05

        def _mock_fused_moe(x, selected_experts, routing_weights, expert_weight):
            y = jnp.einsum('bsh,hd->bsd', x, expert_weight)
            scale = routing_weights.sum(axis=-1, keepdims=True)
            return y * scale
        residuals = hidden_states
        logits = jnp.einsum('bsh,he->bse', hidden_states, gate_w)
        routing_weights, selected_experts = jax.lax.top_k(logits, TOPK)
        h = jnp.einsum('bsh,hi->bsi', residuals, up_w)
        h = jnp.square(jax.nn.relu(h))
        shared_out = jnp.einsum('bsi,ih->bsh', h, down_w)
        moe_out = _mock_fused_moe(hidden_states, selected_experts, routing_weights, expert_weight)
        y = shared_out + moe_out
        mu = y.mean(axis=-1, keepdims=True)
        var = jnp.mean(jnp.square(y - mu), axis=-1, keepdims=True)
        return (y - mu) * jax.lax.rsqrt(var + EPS) * ln_gamma + ln_beta
    x = x + jnp.tanh(g_xattn[0]) * _L0_xattn_ref(_layernorm(x, axis=-1), ctx_2048, L0_xattn_q_w, L0_xattn_q_b, L0_xattn_k_w, L0_xattn_k_b, L0_xattn_v_w, L0_xattn_v_b, L0_xattn_k_img_w, L0_xattn_k_img_b, L0_xattn_v_img_w, L0_xattn_v_img_b, L0_xattn_o_w, L0_xattn_o_b, L0_xattn_norm_q_w, L0_xattn_norm_k_w, L0_xattn_norm_k_img_w)
    x = x + jnp.tanh(g_ffn[0]) * _L0_ffn_ref(_layernorm(x, axis=-1), L0_ffn_gate_w, L0_ffn_up_w, L0_ffn_down_w, L0_ffn_expert_weight, L0_ffn_ln_gamma, L0_ffn_ln_beta)
    return x

_drawn_inputs = setup_inputs


def setup_inputs(seed=0):
    import zlib

    import numpy as np

    out = dict(_drawn_inputs(seed))
    spreads = {'L0_xattn_q_b': (0.0, 0.709),
     'L0_xattn_k_b': (0.0, 0.1),
     'L0_xattn_v_b': (0.0, 0.1),
     'L0_xattn_k_img_b': (0.0, 0.8),
     'L0_xattn_v_img_b': (0.0, 0.1),
     'L0_xattn_o_b': (0.0, 0.1),
     'L0_xattn_norm_q_w': (1.0, 0.6),
     'L0_xattn_norm_k_w': (1.0, 0.2),
     'L0_xattn_norm_k_img_w': (1.0, 0.6),
     'L0_ffn_ln_gamma': (1.0, 0.2),
     'L0_ffn_ln_beta': (0.0, 0.1)}
    factors = {}
    for name, (base, spread) in spreads.items():
        noise = np.random.default_rng([zlib.crc32(name.encode()), seed]).standard_normal(out[name].shape)
        drawn = base * np.exp(spread * noise) if base else spread * noise
        out[name] = jnp.asarray(drawn.astype(out[name].dtype))
    for name, factor in factors.items():
        out[name] = (out[name] * factor).astype(out[name].dtype)
    return out
```

```python
from contextlib import ExitStack

import concourse.bass as bass
from concourse import mybir

F32 = mybir.dt.float32
F32R = mybir.dt.float32r
ALU = mybir.AluOpType
ACT = mybir.ActivationFunctionType
AX = mybir.AxisListType

P = 128
D = 512
KT = D // P
NH = 16
HD = D // NH
HG = P // HD
NG = NH // HG
EPS_LN = 1e-5
EPS_RMS = 1e-6
DMA = 16


def flamingo_layer(nc, t, out):
    NB = t["x"].shape[0]
    INTER = t["down"].shape[1] // D * P
    NI = INTER // P
    NE = t["gate"].shape[1] // KT
    GB = D // P
    NGRP = NB // GB

    x2_dram = nc.dram_tensor("x2_scratch", [NB, P, D], F32, kind="Internal").ap()

    def at_least(eng, sem, value, apart=False):
        if isinstance(value, int) and value <= 0:
            return
        eng.wait_ge(sem, value)
        if apart and not isinstance(value, int):
            eng.sem_inc(passed[eng], 1)

    with ExitStack() as whole:
        def sem(name):
            return whole.enter_context(nc.semaphore(name))

        def sb(ctx, name, shape, dt=F32):
            return ctx.enter_context(nc.sbuf_tensor(name, shape, dt))

        bank = [whole.enter_context(nc.psum_tensor(f"bank{n}", [P, D], F32)) for n in range(8)]
        ident = sb(whole, "ident", [P, P])
        gains = sb(whole, "gains", [P, 2])
        tanh_g = sb(whole, "tanh_g", [P, 2])
        powers = sb(whole, "powers", [P, 1 + HG])

        s_const = sem("constants_loaded")
        n_const = DMA * 3
        passed = {e: sem(f"passed_{n}") for n, e in enumerate((nc.sync, nc.tensor, nc.vector, nc.gpsimd))}
        s_tanh = sem("tanh_done")
        s_pow = sem("powers_set")

        def mm3(eng, dst, stat, mov, first=True, last=True):
            n = len(stat)
            for k, ((ah, al), (bh, bl)) in enumerate(zip(stat, mov)):
                eng.matmul(dst, ah, bh, start=first and k == 0, stop=False)
                eng.matmul(dst, ah, bl, start=False, stop=False)
                mm = eng.matmul(dst, al, bh, start=False, stop=last and k == n - 1)
            return mm

        with ExitStack() as ctx:
            W = {n: (sb(ctx, n + "_hi", [P, KT, D], F32R), sb(ctx, n + "_lo", [P, KT, D], F32R))
                 for n in ("wk", "wq", "wv", "wo")}
            bk = sb(ctx, "bk", [P, D])
            bq = sb(ctx, "bq", [P, D])
            bv = sb(ctx, "bv", [P, D])
            tgbo = sb(ctx, "tgbo", [P, D])
            nqk = sb(ctx, "nqk", [P, D])
            xin = [sb(ctx, f"xin{n}", [P, D]) for n in range(2)]
            cin = [sb(ctx, f"cin{n}", [P, D]) for n in range(2)]
            xres = [sb(ctx, f"xres{n}", [P, D]) for n in range(2)]
            x2 = [sb(ctx, f"x2_{n}", [P, D]) for n in range(2)]
            xn = sb(ctx, "xn", [P, D])
            xnT_hi, xnT_lo = sb(ctx, "xnT_hi", [P, D], F32R), sb(ctx, "xnT_lo", [P, D], F32R)
            cT_hi, cT_lo = sb(ctx, "cT_hi", [P, D], F32R), sb(ctx, "cT_lo", [P, D], F32R)
            kb, qb, vb = sb(ctx, "kb", [P, D]), sb(ctx, "qb", [P, D]), sb(ctx, "vb", [P, D])
            kf = sb(ctx, "kf", [P, D])
            junk_k, junk_q = sb(ctx, "junk_k", [P, D]), sb(ctx, "junk_q", [P, D])
            v_hi, v_lo = sb(ctx, "v_hi", [P, D], F32R), sb(ctx, "v_lo", [P, D], F32R)
            qT_hi, qT_lo = sb(ctx, "qT_hi", [P, D], F32R), sb(ctx, "qT_lo", [P, D], F32R)
            kd_hi = sb(ctx, "kd_hi", [P, NG, HG, P], F32R)
            kd_lo = sb(ctx, "kd_lo", [P, NG, HG, P], F32R)
            prob = sb(ctx, "prob", [P, NG, HG * P])
            pT_hi, pT_lo = sb(ctx, "pT_hi", [P, NG, HG * P], F32R), sb(ctx, "pT_lo", [P, NG, HG * P], F32R)
            aT_hi, aT_lo = sb(ctx, "aT_hi", [P, NG, P], F32R), sb(ctx, "aT_lo", [P, NG, P], F32R)
            st6, mv = sb(ctx, "st6", [P, 6]), sb(ctx, "mv", [P, 2])
            var, rstd = sb(ctx, "var", [P, 1]), sb(ctx, "rstd", [P, 1])
            ssk, ssq = sb(ctx, "ssk", [P, 1]), sb(ctx, "ssq", [P, 1])
            mk, mq = sb(ctx, "mk", [P, 1]), sb(ctx, "mq", [P, 1])
            rk, rq = sb(ctx, "rk", [P, 1]), sb(ctx, "rq", [P, 1])
            mx, nb = sb(ctx, "mx", [P, NH]), sb(ctx, "nb", [P, NH])
            rs, rr = sb(ctx, "rs", [P, NH]), sb(ctx, "rr", [P, NH])
            stage = [prob[:, :, :].rearrange("p g n -> p (g n)"), kb, ]

            ld_w, ld_b = [sem(f"ld_w{n}") for n in range(4)], sem("ld_b")
            ld_x, ld_c, ld_r, st_x2 = ([sem(f"{s}{n}") for n in range(2)] for s in ("ld_x", "ld_c", "ld_r", "st_x2_"))
            wh, wl, cst, kdz = sem("weights_hi"), sem("weights_lo"), sem("row_consts"), sem("kd_zero")
            pe_K, pe_Q, pe_Tx, pe_TP, pe_PV, pe_V, pe_Tk, pe_Tq, pe_S, pe_O = (
                sem("pe_" + n) for n in ("K", "Q", "Tx", "TP", "PV", "V", "Tk", "Tq", "S", "O"))
            dv_kb, dv_qb, dv_kf, dv_xT, dv_pT, dv_aT, dv_vb, dv_kT, dv_qT, dv_mx, dv_nb, dv_x2, dv_bs, dv_st = (
                sem("dv_" + n) for n in ("kb", "qb", "kf", "xT", "pT", "aT", "vb", "kT", "qT", "mx", "nb", "x2", "bs", "st"))
            ac_sk, ac_sq, ac_xT, ac_pT, ac_aT, ac_v, ac_kT, ac_qT, ac_c, ac_e = (
                sem("ac_" + n) for n in ("sk", "sq", "xT", "pT", "aT", "v", "kT", "qT", "c", "e"))
            po_mk, po_rk, po_mq, po_rq, po_v, po_c, po_r, po_var, po_rs, po_xn, po_rr, po_p = (
                sem("po_" + n) for n in ("mk", "rk", "mq", "rq", "v", "c", "r", "var", "rs", "xn", "rr", "p"))

            def has(b):
                return not isinstance(b, int) or 0 <= b < NB

            def run(eng, slot, before=None, after=None):
                if before:
                    before()
                for b in range(3):
                    slot(b, b % 2)
                with eng.Fori(0, (NB - 6) // 2) as i:
                    for j in range(2):
                        slot(i * 2 + (3 + j), (3 + j) % 2)
                for b in range(NB - 3, NB + 1):
                    slot(b, b % 2)
                if after:
                    after()

            def parity_count(b, par):
                return (b - par) // 2 * DMA + DMA if isinstance(b, int) else (b - par) * (DMA // 2) + DMA

            def cols(a, k):
                return a[:, k * P:(k + 1) * P]

            block = ctx.enter_context(nc.Block())

            @block.sync
            def _(sp):
                def load(b, par, src, dst, s):
                    sp.dma_start(dst[par][:, :], src[b]).then_inc(s[par], DMA)

                def before():
                    sp.dma_start(ident[:, :], t["ident"]).then_inc(s_const, DMA)
                    for n in range(2):
                        sp.dma_start(gains[:, n:n + 1], t[("g_xattn", "g_ffn")[n]].broadcast_to([P, 1])).then_inc(s_const, DMA)
                    load(0, 0, t["x"], xin, ld_x)
                    load(0, 0, t["ctxT"], cin, ld_c)
                    for n, name in enumerate(("wk", "wq", "wv", "wo")):
                        if n:
                            sp.wait_ge(wl, n)
                        sp.dma_start(prob[:, :, :], t[name].rearrange("p (k n) -> p k n", k=KT)).then_inc(ld_w[n], DMA)
                        if n == 0:
                            for dst, src in ((bk, "bk"), (bq, "bq"), (bv, "bv"), (tgbo, "bo"), (nqk, "nq"), (junk_k, "nk")):
                                sp.dma_start(dst[:, :], t[src].broadcast_to([P, D])).then_inc(ld_b, DMA)
                            load(1, 1, t["x"], xin, ld_x)
                            load(1, 1, t["ctxT"], cin, ld_c)
                    sp.wait_ge(po_xn, 1)
                    load(2, 0, t["x"], xin, ld_x)

                def slot(b, par):
                    if has(b) and has(b + 3):
                        at_least(sp, po_xn, b + 2, apart=True)
                        load(b + 3, 1 - par, t["x"], xin, ld_x)
                    if has(b) and has(b + 2):
                        at_least(sp, ac_c, b + 1, apart=True)
                        at_least(sp, po_c, b + 1, apart=True)
                        load(b + 2, par, t["ctxT"], cin, ld_c)
                    if has(b):
                        at_least(sp, st_x2[par], parity_count(b - 2, par) if has(b - 2) else 0, apart=True)
                        at_least(sp, dv_x2, b - 1, apart=True)
                        load(b, par, t["x"], xres, ld_r)
                    if has(b - 1):
                        at_least(sp, dv_x2, b, apart=True)
                        sp.dma_start(x2_dram[b - 1], x2[1 - par][:, :]).then_inc(st_x2[1 - par], DMA)

                def after():
                    for n in range(2):
                        sp.wait_ge(st_x2[n], NB // 2 * DMA)

                run(sp, slot, before, after)

            @block.tensor
            def _(pe):
                wk, wq, wv, wo = ([(h[:, k, :], l[:, k, :]) for k in range(KT)] for h, l in (W[n] for n in ("wk", "wq", "wv", "wo")))
                cT = [(cols(cT_hi, k), cols(cT_lo, k)) for k in range(KT)]
                xT = [(cols(xnT_hi, k), cols(xnT_lo, k)) for k in range(KT)]

                def turn(src, dst, s):
                    for k in range(KT):
                        mm = pe.transpose(cols(dst, k), cols(src, k), ident[:, :])
                    mm.then_inc(s, 1)

                def turn_x(b):
                    at_least(pe, dv_x2, b - 2)
                    at_least(pe, po_xn, b + 1)
                    turn(xn, bank[6], pe_Tx)

                def before():
                    pe.wait_ge(s_const, n_const)
                    turn_x(0)

                def slot(b, par):
                    a = b - 1
                    if has(b):
                        if isinstance(b, int) and b == 0:
                            pe.wait_ge(wh, 1)
                            pe.wait_ge(wl, 1)
                        at_least(pe, ac_c, b + 1)
                        at_least(pe, po_c, b + 1)
                        mm3(pe, bank[4][:, :], cT, wk).then_inc(pe_K, 1)
                        if isinstance(b, int) and b == 0:
                            pe.wait_ge(wh, 2)
                            pe.wait_ge(wl, 2)
                        at_least(pe, ac_xT, b + 1)
                        at_least(pe, dv_xT, b + 1)
                        mm3(pe, bank[5][:, :], xT, wq).then_inc(pe_Q, 1)
                        if has(b + 1):
                            turn_x(b + 1)
                    if has(a):
                        def turn_probs(g):
                            if g == 0:
                                at_least(pe, dv_vb, a + 1)
                            if has(b) and g == 1:
                                at_least(pe, dv_kb, b + 1)
                            if has(b) and g == 2:
                                at_least(pe, dv_qb, b + 1)
                            if g == 3 and has(b) and has(b + 1):
                                at_least(pe, ac_xT, b + 2)
                                at_least(pe, dv_xT, b + 2)
                            at_least(pe, po_p, a * NG + (g + 1))
                            for h in range(HG):
                                mm = pe.transpose(cols(bank[(7, 4, 5, 6)[g]], h), prob[:, g, h * P:(h + 1) * P], ident[:, :])
                            mm.then_inc(pe_TP, 1)

                        turn_probs(0)
                        for g in range(NG):
                            if g + 1 < NG:
                                turn_probs(g + 1)
                            if g == 0:
                                at_least(pe, ac_v, a + 1)
                                at_least(pe, po_v, a + 1)
                            at_least(pe, ac_pT, a * NG + (g + 1))
                            at_least(pe, dv_pT, a * NG + (g + 1))
                            mm = mm3(pe, bank[g][:, :], [(cols(v_hi, g), cols(v_lo, g))], [(pT_hi[:, g, :], pT_lo[:, g, :])])
                        mm.then_inc(pe_PV, 1)
                    if has(b):
                        if isinstance(b, int) and b == 0:
                            pe.wait_ge(wh, 3)
                            pe.wait_ge(wl, 3)
                        mm3(pe, bank[7][:, :], cT, wv).then_inc(pe_V, 1)
                        at_least(pe, dv_kf, b + 1)
                        turn(kf, bank[4], pe_Tk)
                        turn(qb, bank[5], pe_Tq)
                    if has(a):
                        at_least(pe, ac_aT, a + 1)
                        at_least(pe, dv_aT, a + 1)
                    if has(b):
                        at_least(pe, ac_kT, b + 1)
                        at_least(pe, dv_kT, b + 1)
                        at_least(pe, ac_qT, b + 1)
                        at_least(pe, dv_qT, b + 1)
                        for g in range(NG):
                            mm3(pe, bank[g][:, :], [(cols(qT_hi, g), cols(qT_lo, g))],
                                [(kd_hi[:, g, :, :].rearrange("p h k -> p (h k)"), kd_lo[:, g, :, :].rearrange("p h k -> p (h k)"))]).then_inc(pe_S, 1)
                    if has(a):
                        if isinstance(b, int) and a == 0:
                            pe.wait_ge(wh, 4)
                            pe.wait_ge(wl, 4)
                        mm3(pe, bank[6][:, :], [(aT_hi[:, g, :], aT_lo[:, g, :]) for g in range(NG)], wo).then_inc(pe_O, 1)

                run(pe, slot, before)

            @block.vector
            def _(dve):
                def stats(b, par):
                    at_least(dve, ld_x[par], parity_count(b, par))
                    at_least(dve, po_rs, b)
                    at_least(dve, po_xn, b)
                    dve.bn_stats(st6[:, :], xin[par][:, :]).then_inc(dv_bs, 1)
                    at_least(dve, dv_bs, b + 1, apart=True)
                    dve.bn_aggr(mv[:, :], st6[:, :]).then_inc(dv_st, 1)

                def split_xT(b):
                    at_least(dve, ac_xT, b + 1)
                    dve.tensor_tensor(xnT_lo[:, :], bank[6][:, :], xnT_hi[:, :].bitcast(F32), ALU.subtract).then_inc(dv_xT, 1)

                def before():
                    dve.memset(kd_hi[:, :, :, :].bitcast(mybir.dt.uint32), 0).then_inc(kdz, 1)
                    dve.memset(kd_lo[:, :, :, :].bitcast(mybir.dt.uint32), 0).then_inc(kdz, 1)
                    stats(0, 0)
                    for n, name in enumerate(("wk", "wq", "wv", "wo")):
                        dve.wait_ge(wh, n + 1)
                        dve.tensor_tensor(W[name][1][:, :, :], prob[:, :, :], W[name][0][:, :, :].bitcast(F32), ALU.subtract).then_inc(wl, 1)
                        if n == 0:
                            dve.wait_ge(ld_b, 6 * DMA)
                            dve.tensor_tensor(nqk[:, :], nqk[:, :], junk_k[:, :], ALU.mult).then_inc(cst, 1)
                            dve.wait_ge(s_tanh, 1)
                            dve.tensor_scalar(tgbo[:, :], tgbo[:, :], tanh_g[:, 0:1], None, ALU.mult).then_inc(cst, 1)
                            split_xT(0)
                            stats(1, 1)
                    dve.wait_ge(cst, 2)

                def slot(b, par):
                    a = b - 1
                    if has(b):
                        at_least(dve, pe_K, b + 1)
                        dve.tensor_tensor(kb[:, :], bank[4][:, :], bk[:, :], ALU.add).then_inc(dv_kb, 1)
                        at_least(dve, pe_Q, b + 1)
                        dve.tensor_tensor(qb[:, :], bank[5][:, :], bq[:, :], ALU.add).then_inc(dv_qb, 1)
                        at_least(dve, po_rk, b + 1)
                        dve.scalar_tensor_tensor(out=kf[:, :], in0=kb[:, :], scalar=rk[:, 0:1], in1=nqk[:, :],
                                                 op0=ALU.mult, op1=ALU.mult).then_inc(dv_kf, 1)
                        if has(b + 1):
                            split_xT(b + 1)
                    if has(a):
                        for g in range(NG):
                            at_least(dve, ac_pT, a * NG + (g + 1))
                            dve.tensor_tensor(pT_lo[:, g, :], bank[(7, 4, 5, 6)[g]][:, :], pT_hi[:, g, :].bitcast(F32), ALU.subtract).then_inc(dv_pT, 1)
                        at_least(dve, ac_aT, a + 1)
                        for h in range(HG):
                            q = slice(h * HD, (h + 1) * HD)
                            for g in range(NG):
                                i = dve.tensor_tensor(aT_lo[q, g, :], bank[g][q, h * P:(h + 1) * P], aT_hi[q, g, :].bitcast(F32), ALU.subtract)
                        i.then_inc(dv_aT, 1)
                    if has(b):
                        at_least(dve, pe_V, b + 1)
                        at_least(dve, po_v, b)
                        dve.tensor_tensor(vb[:, :], bank[7][:, :], bv[:, :], ALU.add).then_inc(dv_vb, 1)
                        at_least(dve, ac_kT, b + 1)
                        for h in range(HG):
                            q = slice(h * HD, (h + 1) * HD)
                            i = dve.tensor_tensor(kd_lo[q, :, h, :], bank[4][q, :].rearrange("p (g k) -> p g k", g=NG),
                                                  kd_hi[q, :, h, :].bitcast(F32), ALU.subtract)
                        i.then_inc(dv_kT, 1)
                        at_least(dve, ac_qT, b + 1)
                        dve.tensor_tensor(qT_lo[:, :], bank[5][:, :], qT_hi[:, :].bitcast(F32), ALU.subtract).then_inc(dv_qT, 1)
                        at_least(dve, po_rq, b + 1)
                        for g in range(NG):
                            hs = slice(g * HG, (g + 1) * HG)
                            at_least(dve, pe_S, b * NG + (g + 1))
                            dve.tensor_reduce(mx[:, hs], bank[g][:, :].rearrange("p (h k) -> p h k", h=HG), AX.X, ALU.max).then_inc(dv_mx, 1)
                            at_least(dve, dv_mx, b * NG + (g + 1))
                            dve.tensor_scalar(nb[:, hs], mx[:, hs], rq[:, 0:1], -1.0, ALU.mult, ALU.mult).then_inc(dv_nb, 1)
                    if has(a):
                        at_least(dve, po_r, a + 1)
                        if has(a - 2):
                            at_least(dve, st_x2[1 - par], parity_count(a - 2, 1 - par))
                        at_least(dve, pe_O, a + 1)
                        dve.scalar_tensor_tensor(out=x2[1 - par][:, :], in0=bank[6][:, :], scalar=tanh_g[:, 0:1],
                                                 in1=xres[1 - par][:, :], op0=ALU.mult, op1=ALU.add).then_inc(dv_x2, 1)
                    if has(b) and has(b + 2):
                        stats(b + 2, par)

                run(dve, slot, before)

            @block.scalar
            def _(act):
                def copy(dst, src):
                    return act.activation(dst, src, ACT.Copy)

                def hi_xT(b):
                    at_least(act, pe_Tx, b + 1)
                    copy(xnT_hi[:, :], bank[6][:, :]).then_inc(ac_xT, 1)

                def hi_ctx(b, par):
                    at_least(act, ld_c[par], parity_count(b, par))
                    at_least(act, pe_V, b)
                    copy(cT_hi[:, :], cin[par][:, :]).then_inc(ac_c, 1)

                def before():
                    act.wait_ge(s_const, n_const)
                    act.activation(tanh_g[:, :], gains[:, :], ACT.Tanh).then_inc(s_tanh, 1)
                    hi_ctx(0, 0)
                    for n, name in enumerate(("wk", "wq", "wv", "wo")):
                        act.wait_ge(ld_w[n], DMA)
                        copy(W[name][0][:, :, :], prob[:, :, :]).then_inc(wh, 1)
                        if n == 0:
                            hi_xT(0)
                    act.wait_ge(kdz, 2)
                    act.wait_ge(wl, 4)
                    act.wait_ge(cst, 2)

                def exps(b, g):
                    at_least(act, dv_nb, b * NG + (g + 1))
                    at_least(act, po_rr, b * NG + (g + 1) - NG)
                    for h in range(HG):
                        n = g * HG + h
                        i = act.activation(prob[:, g, h * P:(h + 1) * P], cols(bank[g], h), ACT.Exp,
                                           bias=nb[:, n:n + 1], scale=rq[:, 0:1], accum_out=rs[:, n:n + 1])
                    i.then_inc(ac_e, 1)

                def slot(b, par):
                    a = b - 1
                    if has(a):
                        exps(a, 0)
                        exps(a, 1)
                    if has(b):
                        at_least(act, dv_kb, b + 1)
                        at_least(act, po_mk, b)
                        act.activation(junk_k[:, :], kb[:, :], ACT.Square, accum_out=ssk[:, :]).then_inc(ac_sk, 1)
                    if has(a):
                        exps(a, 2)
                        exps(a, 3)
                    if has(b):
                        at_least(act, dv_qb, b + 1)
                        at_least(act, po_mq, b)
                        act.activation(junk_q[:, :], qb[:, :], ACT.Square, accum_out=ssq[:, :]).then_inc(ac_sq, 1)
                        if has(b + 1):
                            hi_xT(b + 1)
                    if has(a):
                        for g in range(NG):
                            at_least(act, pe_TP, a * NG + (g + 1))
                            copy(pT_hi[:, g, :], bank[(7, 4, 5, 6)[g]][:, :]).then_inc(ac_pT, 1)
                        at_least(act, pe_PV, a + 1)
                        for h in range(HG):
                            q = slice(h * HD, (h + 1) * HD)
                            for g in range(NG):
                                i = copy(aT_hi[q, g, :], bank[g][q, h * P:(h + 1) * P])
                        i.then_inc(ac_aT, 1)
                    if has(b):
                        at_least(act, dv_vb, b + 1)
                        copy(v_hi[:, :], vb[:, :]).then_inc(ac_v, 1)
                        at_least(act, pe_Tk, b + 1)
                        for h in range(HG):
                            q = slice(h * HD, (h + 1) * HD)
                            i = copy(kd_hi[q, :, h, :], bank[4][q, :].rearrange("p (g k) -> p g k", g=NG))
                        i.then_inc(ac_kT, 1)
                        at_least(act, pe_Tq, b + 1)
                        copy(qT_hi[:, :], bank[5][:, :]).then_inc(ac_qT, 1)
                        if has(b + 1):
                            hi_ctx(b + 1, 1 - par)

                run(act, slot, before)

            @block.gpsimd
            def _(pool):
                def inv_rms(b, ss, m, r, got, s_m, s_r, scale):
                    at_least(pool, got, b + 1, apart=True)
                    pool.tensor_scalar(m[:, :], ss[:, :], scale / D, scale * EPS_RMS, ALU.mult, ALU.add).then_inc(s_m, 1)
                    at_least(pool, s_m, b + 1)
                    pool.tensor_tensor(r[:, :], m[:, :], powers[:, 0:1], ALU.pow).then_inc(s_r, 1)

                def lo_ctx(b, par):
                    at_least(pool, ac_c, b + 1)
                    pool.tensor_tensor(cT_lo[:, :], cin[par][:, :], cT_hi[:, :].bitcast(F32), ALU.subtract).then_inc(po_c, 1)

                def normalise(b, par):
                    at_least(pool, dv_st, b + 1, apart=True)
                    pool.tensor_scalar(var[:, :], mv[:, 1:2], EPS_LN, None, ALU.add).then_inc(po_var, 1)
                    at_least(pool, po_var, b + 1)
                    pool.tensor_tensor(rstd[:, :], var[:, :], powers[:, 0:1], ALU.pow).then_inc(po_rs, 1)
                    at_least(pool, po_rs, b + 1)
                    at_least(pool, pe_Tx, b, apart=True)
                    pool.tensor_scalar(xn[:, :], xin[par][:, :], mv[:, 0:1], rstd[:, 0:1], ALU.subtract, ALU.mult).then_inc(po_xn, 1)

                def divide(b, g):
                    hs = slice(g * HG, (g + 1) * HG)
                    at_least(pool, ac_e, b * NG + (g + 1))
                    pool.tensor_tensor(rr[:, hs], rs[:, hs], powers[:, 1:], ALU.pow).then_inc(po_rr, 1)
                    at_least(pool, po_rr, b * NG + (g + 1))
                    p = prob[:, g, :].rearrange("p (h k) -> p h k", h=HG)
                    pool.tensor_tensor(p, p, rr[:, hs].unsqueeze(2).broadcast_to([P, HG, P]), ALU.mult).then_inc(po_p, 1)

                def before():
                    pool.memset(powers[:, 0:1], -0.5).then_inc(s_pow, 1)
                    pool.memset(powers[:, 1:], -1.0).then_inc(s_pow, 1)
                    lo_ctx(0, 0)
                    pool.wait_ge(s_pow, 2)
                    normalise(0, 0)
                    normalise(1, 1)

                def slot(b, par):
                    a = b - 1
                    if has(a):
                        divide(a, 0)
                        divide(a, 1)
                    if has(b):
                        inv_rms(b, ssk, mk, rk, ac_sk, po_mk, po_rk, 1.0)
                    if has(a):
                        divide(a, 2)
                        divide(a, 3)
                    if has(b):
                        inv_rms(b, ssq, mq, rq, ac_sq, po_mq, po_rq, float(HD))
                        at_least(pool, ac_v, b + 1)
                        pool.tensor_tensor(v_lo[:, :], vb[:, :], v_hi[:, :].bitcast(F32), ALU.subtract).then_inc(po_v, 1)
                        if has(b + 1):
                            lo_ctx(b + 1, 1 - par)
                        if isinstance(b, int) and b == 0:
                            pool.wait_ge(cst, 2)
                        at_least(pool, ld_r[par], parity_count(b, par))
                        pool.tensor_tensor(xres[par][:, :], xres[par][:, :], tgbo[:, :], ALU.add).then_inc(po_r, 1)
                        if has(b + 2):
                            normalise(b + 2, par)

                run(pool, slot, before)

            del block

        with ExitStack() as ctx:
            feed_forward(nc, ctx, t, out, x2_dram, bank, ident, tanh_g, powers, s_const, n_const, at_least, mm3)


def feed_forward(nc, ctx, t, out, x2_dram, bank, ident, tanh_g, powers, s_const, n_const, at_least, mm3):
    NB = t["x"].shape[0]
    NI = t["down"].shape[1] // D
    NE = t["gate"].shape[1] // KT
    GB = D // P
    NGRP = NB // GB

    def sb(name, shape, dt=F32):
        return ctx.enter_context(nc.sbuf_tensor(name, shape, dt))

    def sem(name):
        return ctx.enter_context(nc.semaphore(name))

    up_hi, up_lo = sb("up_hi", [P, NI, KT * P], F32R), sb("up_lo", [P, NI, KT * P], F32R)
    dn_hi, dn_lo = sb("dn_hi", [P, NI, D], F32R), sb("dn_lo", [P, NI, D], F32R)
    ex_hi, ex_lo = sb("ex_hi", [P, KT, D], F32R), sb("ex_lo", [P, KT, D], F32R)
    ga_hi, ga_lo = sb("ga_hi", [P, KT * NE], F32R), sb("ga_lo", [P, KT * NE], F32R)
    ga_raw = sb("ga_raw", [P, KT * NE])
    xT_hi, xT_lo = sb("fxT_hi", [P, KT, D], F32R), sb("fxT_lo", [P, KT, D], F32R)
    hT_hi = [sb(f"hT_hi{n}", [P, D], F32R) for n in range(2)]
    hT_lo = [sb(f"hT_lo{n}", [P, D], F32R) for n in range(2)]
    relu, hid = sb("relu", [P, D]), sb("hid", [P, D])
    xin = [sb(f"fxin{n}", [P, D]) for n in range(2)]
    xn = [sb(f"fxn{n}", [P, D]) for n in range(2)]
    moe = [sb(f"moe{n}", [P, D]) for n in range(2)]
    y = [sb(f"y{n}", [P, D]) for n in range(GB)]
    res = [sb(f"fres{n}", [P, D]) for n in range(2)]
    gamma, beta = sb("gamma", [P, D]), sb("beta", [P, D])
    lg = sb("lg", [NE, D])
    top, route = sb("top", [P, GB, 8]), sb("route", [P, GB])
    st6, mv, var, rstd = sb("fst6", [P, 6]), sb("fmv", [P, 2]), sb("fvar", [P, 1]), sb("frstd", [P, 1])
    yvar = sb("yvar", [P, GB])
    yst6, ymv, yrstd = sb("yst6", [P, GB, 6]), sb("ymv", [P, GB, 2]), sb("yrstd", [P, GB])
    nstage = 4
    stage = y

    ld_s = [sem(f"ld_s{n}") for n in range(nstage)]
    fh, fl, fcst, ld_g = sem("f_hi"), sem("f_lo"), sem("f_consts"), sem("ld_g")
    ld_x, ld_r, st_o = ([sem(f"f{s}{n}") for n in range(2)] for s in ("ld_x", "ld_r", "st_o"))
    pe_T, pe_G, pe_TG, pe_U, pe_D, pe_E = (sem("fpe_" + n) for n in ("T", "G", "TG", "U", "D", "E"))
    ac_T, ac_G, ac_r, ac_h, ac_m = (sem("fac_" + n) for n in ("T", "G", "r", "h", "m"))
    dv_T, dv_bs, dv_st, dv_top, dv_s, dv_h, dv_l, dv_y, dv_yb, dv_ys, dv_a, dv_o = (
        sem("fdv_" + n) for n in ("T", "bs", "st", "top", "s", "h", "l", "y", "yb", "ys", "a", "o"))
    po_var, po_rs, po_xn, po_r, po_yv, po_ys = (sem("fpo_" + n) for n in ("var", "rs", "xn", "r", "yv", "ys"))

    def run(eng, group, before=None, after=None):
        if before:
            before()
        group(0)
        with eng.Fori(1, NGRP - 1) as i:
            group(i)
        group(NGRP - 1)
        if after:
            after()

    def static(g):
        return isinstance(g, int)

    def half(n, c):
        return n * (GB // 2 * DMA) + (c // 2 + 1) * DMA

    pieces = [(t["up"].rearrange("p (i n) -> p i n", i=NI)[:, i, :], up_hi[:, i, :], up_lo[:, i, :]) for i in range(NI)]
    pieces += [(t["down"].rearrange("p (i n) -> p i n", i=NI)[:, i, :], dn_hi[:, i, :], dn_lo[:, i, :]) for i in range(NI)]
    order = [n for i in range(NI) for n in (i, NI + i)]
    pieces = [pieces[n] for n in order]
    pieces += [(t["ex"].rearrange("p (k n) -> p k n", k=KT)[:, k, :], ex_hi[:, k, :], ex_lo[:, k, :]) for k in range(KT)]

    block = ctx.enter_context(nc.Block())

    @block.sync
    def _(sp):
        def load_x(g, j):
            sp.dma_start(xin[j % 2][:, :], x2_dram[g * GB + j]).then_inc(ld_x[j % 2], DMA)

        def before():
            for src, dst in (("gamma", gamma), ("beta", beta)):
                sp.dma_start(dst[:, :], t[src].broadcast_to([P, D])).then_inc(ld_g, DMA)
            sp.dma_start(ga_raw[:, :], t["gate"]).then_inc(ld_g, DMA)
            for n in range(2):
                sp.sem_inc(st_o[n], DMA)
            load_x(0, 0)
            load_x(0, 1)
            for n, (src, _, _) in enumerate(pieces):
                sp.wait_ge(fl, n - nstage + 2) if n >= nstage else None
                sp.dma_start(stage[n % nstage][:, :], src).then_inc(ld_s[n % nstage], DMA)
                if n == 1:
                    for j in (2, 3):
                        sp.wait_ge(po_xn, j - 1)
                        load_x(0, j)

        def group(g):
            last = static(g) and g == NGRP - 1
            for j in range(GB):
                if j == 2 and not (static(g) and g == 0):
                    finish(g - 1)
                if not last:
                    at_least(sp, po_xn, g * GB + (GB + j - 1), apart=True)
                    load_x(g + 1, j)

        def finish(g):
            for j in range(GB):
                sp_res(g, j)
                at_least(sp, dv_o, g * GB + (j + 1), apart=True)
                sp.dma_start(out[g * GB + j], res[j % 2][:, :]).then_inc(st_o[j % 2], DMA)

        def sp_res(g, j):
            at_least(sp, st_o[j % 2], half(g, j), apart=True)
            sp.dma_start(res[j % 2][:, :], x2_dram[g * GB + j]).then_inc(ld_r[j % 2], DMA)

        def after():
            finish(NGRP - 1)
            for n in range(2):
                sp.wait_ge(st_o[n], (NB // 2 + 1) * DMA)

        run(sp, group, before, after)

    @block.tensor
    def _(pe):
        def turn(g, j):
            at_least(pe, po_xn, g * GB + (j + 1))
            if not (static(g) and g == 0 and j == 0):
                if j:
                    at_least(pe, ac_T, g * GB + j)
                    at_least(pe, dv_T, g * GB + j)
                else:
                    at_least(pe, dv_top, g)
            for k in range(KT):
                mm = pe.transpose(bank[7][:, k * P:(k + 1) * P], xn[j % 2][:, k * P:(k + 1) * P], ident[:, :])
            mm.then_inc(pe_T, 1)

        def upward(g, i):
            if static(g) and g == 0:
                pe.wait_ge(fl, 2 * i + 2)
            if i < 2:
                at_least(pe, ac_r, g * NI + (i - 1))
            else:
                at_least(pe, ac_r, g * NI + (i - 1))
            mm3(pe, bank[4 + i % 2][:, :],
                [(up_hi[:, i, k * P:(k + 1) * P], up_lo[:, i, k * P:(k + 1) * P]) for k in range(KT)],
                [(xT_hi[:, k, :], xT_lo[:, k, :]) for k in range(KT)]).then_inc(pe_U, 1)

        def downward(g, i):
            if static(g) and g == 0:
                pe.wait_ge(fl, 2 * i + 3)
            at_least(pe, dv_l, g * NI + (i + 1))
            for j in range(GB):
                c = slice(j * P, (j + 1) * P)
                if i == 0:
                    at_least(pe, dv_y, (g - 1) * GB + (j + 1))
                mm = mm3(pe, bank[j][:, :], [(hT_hi[i % 2][:, c], hT_lo[i % 2][:, c])],
                         [(dn_hi[:, i, :], dn_lo[:, i, :])], first=i == 0, last=i == NI - 1)
            mm.then_inc(pe_D, 1)

        def expert(g, j):
            if static(g) and g == 0 and j == 0:
                pe.wait_ge(fl, len(pieces) + 1)
            c = slice(j * P, (j + 1) * P)
            if j == 0:
                at_least(pe, ac_G, g + 1)
            else:
                at_least(pe, ac_m, g * GB + j)
            mm3(pe, bank[6][:, :], [(xT_hi[:, k, c], xT_lo[:, k, c]) for k in range(KT)],
                [(ex_hi[:, k, :], ex_lo[:, k, :]) for k in range(KT)]).then_inc(pe_E, 1)

        def before():
            for j in range(GB):
                turn(0, j)

        def group(g):
            last = static(g) and g == NGRP - 1
            at_least(pe, ac_T, g * GB + GB)
            at_least(pe, dv_T, g * GB + GB)
            at_least(pe, ac_m, g * GB)
            if static(g) and g == 0:
                pe.wait_ge(fl, 1)
            mm3(pe, bank[6][0:NE, :], [(ga_hi[:, k * NE:(k + 1) * NE], ga_lo[:, k * NE:(k + 1) * NE]) for k in range(KT)],
                [(xT_hi[:, k, :], xT_lo[:, k, :]) for k in range(KT)]).then_inc(pe_G, 1)
            upward(g, 0)
            at_least(pe, ac_G, g + 1, apart=True)
            for j in range(GB):
                mm = pe.transpose(bank[7][:, j * NE:(j + 1) * NE], lg[0:NE, j * P:(j + 1) * P], ident[0:NE, 0:NE])
            mm.then_inc(pe_TG, 1)
            for i in range(1, NI):
                upward(g, i)
                downward(g, i - 1)
            expert(g, 0)
            if not last:
                turn(g + 1, 0)
            downward(g, NI - 1)
            for j in range(1, GB):
                expert(g, j)
                if not last:
                    turn(g + 1, j)

        run(pe, group, before)

    @block.scalar
    def _(act):
        def copy(dst, src):
            return act.activation(dst, src, ACT.Copy)

        def hi_T(g, j):
            at_least(act, pe_T, g * GB + (j + 1))
            copy(xT_hi[:, :, j * P:(j + 1) * P], bank[7][:, :].rearrange("p (k n) -> p k n", k=KT)).then_inc(ac_T, 1)

        def before():
            act.wait_ge(ld_g, 3 * DMA)
            copy(ga_hi[:, :], ga_raw[:, :]).then_inc(fh, 1)
            for n, (_, hi, _) in enumerate(pieces):
                act.wait_ge(ld_s[n % nstage], (n // nstage + 1) * DMA)
                copy(hi, stage[n % nstage][:, :]).then_inc(fh, 1)
                if n < GB:
                    hi_T(0, n)

        def tile_hi(g, i):
            at_least(act, pe_U, g * NI + (i + 1))
            at_least(act, dv_h, g * NI + i)
            act.activation(relu[:, :], bank[4 + i % 2][:, :], ACT.Relu).then_inc(ac_r, 1)
            at_least(act, dv_h, g * NI + (i + 1))
            at_least(act, pe_D, g * NI + (i - 1))
            copy(hT_hi[i % 2][:, :], hid[:, :]).then_inc(ac_h, 1)

        def weigh(g, j):
            at_least(act, dv_s, g + 1)
            at_least(act, pe_E, g * GB + (j + 1))
            at_least(act, dv_y, g * GB + (j - 1))
            act.activation(moe[j % 2][:, :], bank[6][:, :], ACT.Copy, scale=route[:, j:j + 1]).then_inc(ac_m, 1)

        def group(g):
            last = static(g) and g == NGRP - 1
            at_least(act, pe_G, g + 1)
            copy(lg[:, :], bank[6][0:NE, :]).then_inc(ac_G, 1)
            for i in range(NI):
                tile_hi(g, i)
            for j in range(GB):
                weigh(g, j)
                if not last:
                    hi_T(g + 1, j)

        run(act, group, before)

    @block.vector
    def _(dve):
        def stats(g, j):
            at_least(dve, ld_x[j % 2], half(g, j))
            at_least(dve, po_xn, g * GB + j)
            dve.bn_stats(st6[:, :], xin[j % 2][:, :]).then_inc(dv_bs, 1)
            at_least(dve, dv_bs, g * GB + (j + 1), apart=True)
            dve.bn_aggr(mv[:, :], st6[:, :]).then_inc(dv_st, 1)

        def lo_T(g, j):
            c = slice(j * P, (j + 1) * P)
            at_least(dve, ac_T, g * GB + (j + 1))
            dve.tensor_tensor(xT_lo[:, :, c], bank[7][:, :].rearrange("p (k n) -> p k n", k=KT),
                              xT_hi[:, :, c].bitcast(F32), ALU.subtract).then_inc(dv_T, 1)

        def before():
            stats(0, 0)
            stats(0, 1)
            dve.wait_ge(ld_g, 3 * DMA)
            dve.tensor_scalar(gamma[:, :], gamma[:, :], tanh_g[:, 1:2], None, ALU.mult).then_inc(fcst, 1)
            dve.tensor_scalar(beta[:, :], beta[:, :], tanh_g[:, 1:2], None, ALU.mult).then_inc(fcst, 1)
            dve.wait_ge(fh, 1)
            dve.tensor_tensor(ga_lo[:, :], ga_raw[:, :], ga_hi[:, :].bitcast(F32), ALU.subtract).then_inc(fl, 1)
            for n, (_, hi, lo) in enumerate(pieces):
                dve.wait_ge(fh, n + 2)
                dve.tensor_tensor(lo, stage[n % nstage][:, :], hi.bitcast(F32), ALU.subtract).then_inc(fl, 1)
                if n < GB:
                    lo_T(0, n)
                    if n < 2:
                        stats(0, 2 + n)
            dve.wait_ge(fcst, 2)
            dve.wait_ge(fl, len(pieces) + 1)

        def hidden(g, i):
            at_least(dve, ac_h, g * NI + i)
            at_least(dve, dv_l, g * NI + i)
            at_least(dve, ac_r, g * NI + (i + 1))
            dve.tensor_tensor(hid[:, :], relu[:, :], relu[:, :], ALU.mult).then_inc(dv_h, 1)
            at_least(dve, ac_h, g * NI + (i + 1))
            dve.tensor_tensor(hT_lo[i % 2][:, :], hid[:, :], hT_hi[i % 2][:, :].bitcast(F32), ALU.subtract).then_inc(dv_l, 1)

        def routing(g):
            at_least(dve, pe_TG, g + 1)
            at_least(dve, ac_m, g * GB, apart=True)
            for j in range(GB):
                i = dve.max(top[:, j, :], bank[7][:, j * NE:(j + 1) * NE])
            i.then_inc(dv_top, 1)
            at_least(dve, dv_top, g + 1)
            dve.tensor_tensor(route[:, :], top[:, :, 0], top[:, :, 1], ALU.add).then_inc(dv_s, 1)

        def add(g, j):
            at_least(dve, pe_D, g * NI + NI)
            at_least(dve, ac_m, g * GB + (j + 1))
            dve.tensor_tensor(y[j][:, :], bank[j][:, :], moe[j % 2][:, :], ALU.add).then_inc(dv_y, 1)

        def y_stats(g, j):
            at_least(dve, dv_y, g * GB + (j + 1))
            dve.bn_stats(yst6[:, j, :], y[j][:, :]).then_inc(dv_yb, 1)
            at_least(dve, dv_yb, g * GB + (j + 1), apart=True)
            dve.bn_aggr(ymv[:, j, :], yst6[:, j, :]).then_inc(dv_ys, 1)

        def result(g, j):
            at_least(dve, dv_ys, g * GB + (j + 1))
            dve.scalar_tensor_tensor(out=y[j][:, :], in0=y[j][:, :], scalar=ymv[:, j, 0:1], in1=gamma[:, :],
                                     op0=ALU.subtract, op1=ALU.mult).then_inc(dv_a, 1)
            at_least(dve, dv_a, g * GB + (j + 1))
            at_least(dve, po_ys, g * GB + (j + 1))
            at_least(dve, po_r, g * GB + (j + 1))
            dve.scalar_tensor_tensor(out=res[j % 2][:, :], in0=y[j][:, :], scalar=yrstd[:, j:j + 1], in1=res[j % 2][:, :],
                                     op0=ALU.mult, op1=ALU.add).then_inc(dv_o, 1)

        def group(g):
            last = static(g) and g == NGRP - 1
            for i in range(NI):
                hidden(g, i)
                if i == 0:
                    routing(g)
                if not (static(g) and g == 0):
                    if 1 <= i <= GB:
                        y_stats(g - 1, i - 1)
                    if 2 <= i <= GB + 1:
                        result(g - 1, i - 2)
                if not last and i >= 8 and i % 2 == 0 and (i - 8) // 2 < GB:
                    stats(g + 1, (i - 8) // 2)
            if not last:
                lo_T(g + 1, 0)
            add(g, 0)
            for j in range(1, GB):
                if not last:
                    lo_T(g + 1, j)
                add(g, j)

        def after():
            for j in range(GB):
                y_stats(NGRP - 1, j)
                result(NGRP - 1, j)

        run(dve, group, before, after)

    @block.gpsimd
    def _(pool):
        def normalise(g, j):
            at_least(pool, dv_st, g * GB + (j + 1), apart=True)
            pool.tensor_scalar(var[:, :], mv[:, 1:2], EPS_LN, None, ALU.add).then_inc(po_var, 1)
            at_least(pool, po_var, g * GB + (j + 1))
            pool.tensor_tensor(rstd[:, :], var[:, :], powers[:, 0:1], ALU.pow).then_inc(po_rs, 1)
            at_least(pool, pe_T, g * GB + (j - 1))
            at_least(pool, po_rs, g * GB + (j + 1), apart=True)
            pool.tensor_scalar(xn[j % 2][:, :], xin[j % 2][:, :], mv[:, 0:1], rstd[:, 0:1], ALU.subtract, ALU.mult).then_inc(po_xn, 1)

        def scale_y(g, j):
            at_least(pool, dv_ys, g * GB + (j + 1), apart=True)
            pool.tensor_scalar(yvar[:, j:j + 1], ymv[:, j, 1:2], EPS_LN, None, ALU.add).then_inc(po_yv, 1)
            at_least(pool, po_yv, g * GB + (j + 1))
            pool.tensor_tensor(yrstd[:, j:j + 1], yvar[:, j:j + 1], powers[:, 0:1], ALU.pow).then_inc(po_ys, 1)

        def residual(g, j):
            at_least(pool, ld_r[j % 2], half(g, j))
            pool.tensor_tensor(res[j % 2][:, :], res[j % 2][:, :], beta[:, :], ALU.add).then_inc(po_r, 1)

        def before():
            for j in range(GB):
                normalise(0, j)
            pool.wait_ge(fcst, 2)

        def group(g):
            last = static(g) and g == NGRP - 1
            if not (static(g) and g == 0):
                finish(g - 1)
            if not last:
                for j in range(GB):
                    normalise(g + 1, j)

        def finish(g):
            for j in range(GB):
                residual(g, j)
                scale_y(g, j)

        def after():
            finish(NGRP - 1)

        run(pool, group, before, after)


def kernel(**inputs):
    import numpy as np
    import concourse.bacc as bacc
    from concourse.bass_utils import run_bass_kernel_spmd

    def f(name):
        return np.asarray(inputs[name])

    def rows_on_partitions(w):
        return np.ascontiguousarray(w.reshape(-1, P, w.shape[1]).transpose(1, 0, 2).reshape(P, -1))

    ctxt = f("ctx_2048")
    nb = ctxt.shape[0]
    up = f("L0_ffn_up_w")
    arrays = {
        "x": f("x"),
        "ctxT": ctxt.transpose(0, 2, 1).reshape(nb, KT, P, P).transpose(0, 2, 1, 3).reshape(nb, P, KT * P),
        "ident": np.eye(P, dtype=np.float32),
        "g_xattn": f("g_xattn").reshape(1, 1),
        "g_ffn": f("g_ffn").reshape(1, 1),
        "wq": rows_on_partitions(f("L0_xattn_q_w").T),
        "wk": rows_on_partitions(f("L0_xattn_k_img_w").T),
        "wv": rows_on_partitions(f("L0_xattn_v_img_w").T),
        "wo": rows_on_partitions(f("L0_xattn_o_w").T),
        "bq": f("L0_xattn_q_b").reshape(1, D),
        "bk": f("L0_xattn_k_img_b").reshape(1, D),
        "bv": f("L0_xattn_v_img_b").reshape(1, D),
        "bo": f("L0_xattn_o_b").reshape(1, D),
        "nq": f("L0_xattn_norm_q_w").reshape(1, D),
        "nk": f("L0_xattn_norm_k_img_w").reshape(1, D),
        "gate": rows_on_partitions(f("L0_ffn_gate_w")),
        "up": up.reshape(KT, P, -1, P).transpose(1, 2, 0, 3).reshape(P, -1),
        "down": rows_on_partitions(f("L0_ffn_down_w")),
        "ex": rows_on_partitions(f("L0_ffn_expert_weight")),
        "gamma": f("L0_ffn_ln_gamma").reshape(1, D),
        "beta": f("L0_ffn_ln_beta").reshape(1, D),
    }
    arrays = {n: np.ascontiguousarray(a) for n, a in arrays.items()}
    nc = bacc.Bacc("TRN2", target_bir_lowering=False, num_devices=1)
    t = {n: nc.dram_tensor("in_" + n, a.shape, mybir.dt.from_np(a.dtype), kind="ExternalInput").ap() for n, a in arrays.items()}
    out = nc.dram_tensor("out_x", arrays["x"].shape, F32, kind="ExternalOutput").ap()
    flamingo_layer(nc, t, out)
    r = run_bass_kernel_spmd(nc, [{"in_" + n: a for n, a in arrays.items()}], core_ids=[0])
    return r.results[0]["out_x"]
```

```python
from contextlib import ExitStack

import concourse.bass as bass
from concourse import mybir

F32 = mybir.dt.float32
F32R = mybir.dt.float32r
ALU = mybir.AluOpType
ACT = mybir.ActivationFunctionType
AX = mybir.AxisListType

P = 128
D = 512
KT = D // P
NH = 16
HD = D // NH
HG = P // HD
NG = NH // HG
EPS_LN = 1e-5
EPS_RMS = 1e-6
DMA = 16


def flamingo_layer(nc, t, out):
    NB = t["x"].shape[0]
    INTER = t["down"].shape[1] // D * P
    NI = INTER // P
    NE = t["gate"].shape[1] // KT
    GB = D // P
    NGRP = NB // GB

    x2_dram = nc.dram_tensor("x2_scratch", [NB, P, D], F32, kind="Internal").ap()

    def at_least(eng, sem, value, apart=False):
        if isinstance(value, int) and value <= 0:
            return
        eng.wait_ge(sem, value)
        if apart and not isinstance(value, int):
            eng.sem_inc(passed[eng], 1)

    with ExitStack() as whole:
        def sem(name):
            return whole.enter_context(nc.semaphore(name))

        def sb(ctx, name, shape, dt=F32):
            return ctx.enter_context(nc.sbuf_tensor(name, shape, dt))

        wide = whole.enter_context(nc.psum_tensor("wide", [P, NG, D], F32))
        bank = [wide[:, n, :] for n in range(NG)]
        bank += [whole.enter_context(nc.psum_tensor(f"bank{n}", [P, D], F32))[:, :] for n in range(NG, 8)]
        ident = sb(whole, "ident", [P, P])
        gains = sb(whole, "gains", [P, 2])
        tanh_g = sb(whole, "tanh_g", [P, 2])
        powers = sb(whole, "powers", [P, 1])

        s_const = sem("constants_loaded")
        n_const = DMA * 3
        passed = {e: sem(f"passed_{n}") for n, e in enumerate((nc.sync, nc.tensor, nc.vector, nc.gpsimd))}
        s_tanh = sem("tanh_done")
        s_pow = sem("powers_set")

        def mm3(eng, dst, stat, mov, first=True, last=True):
            n = len(stat)
            for k, ((ah, al), (bh, bl)) in enumerate(zip(stat, mov)):
                eng.matmul(dst, ah, bh, start=first and k == 0, stop=False)
                eng.matmul(dst, ah, bl, start=False, stop=False)
                mm = eng.matmul(dst, al, bh, start=False, stop=last and k == n - 1)
            return mm

        with ExitStack() as ctx:
            W = {n: (sb(ctx, n + "_hi", [P, KT, D], F32R), sb(ctx, n + "_lo", [P, KT, D], F32R))
                 for n in ("wk", "wq", "wv", "wo")}
            bk = sb(ctx, "bk", [P, D])
            bq = sb(ctx, "bq", [P, D])
            bv = sb(ctx, "bv", [P, D])
            tgbo = sb(ctx, "tgbo", [P, D])
            nqk = sb(ctx, "nqk", [P, D])
            xin = [sb(ctx, f"xin{n}", [P, D]) for n in range(2)]
            cin = [sb(ctx, f"cin{n}", [P, D]) for n in range(2)]
            xres = [sb(ctx, f"xres{n}", [P, D]) for n in range(2)]
            x2 = [sb(ctx, f"x2_{n}", [P, D]) for n in range(2)]
            xn = sb(ctx, "xn", [P, D])
            xnT_hi, xnT_lo = sb(ctx, "xnT_hi", [P, D], F32R), sb(ctx, "xnT_lo", [P, D], F32R)
            cT_hi, cT_lo = sb(ctx, "cT_hi", [P, D], F32R), sb(ctx, "cT_lo", [P, D], F32R)
            kb, qb, vb = sb(ctx, "kb", [P, D]), sb(ctx, "qb", [P, D]), sb(ctx, "vb", [P, D])
            kf, qf = sb(ctx, "kf", [P, D]), sb(ctx, "qf", [P, D])
            junk_k, junk_q = sb(ctx, "junk_k", [P, D]), sb(ctx, "junk_q", [P, D])
            v_hi, v_lo = sb(ctx, "v_hi", [P, D], F32R), sb(ctx, "v_lo", [P, D], F32R)
            qT_hi, qT_lo = sb(ctx, "qT_hi", [P, D], F32R), sb(ctx, "qT_lo", [P, D], F32R)
            kT = sb(ctx, "kT", [P, 2, NG, P], F32R)
            kd = sb(ctx, "kd", [P, 2, NG, HG, P], F32R)
            prob = sb(ctx, "prob", [P, NG, HG * P])
            pT_hi, pT_lo = sb(ctx, "pT_hi", [P, NG, HG * P], F32R), sb(ctx, "pT_lo", [P, NG, HG * P], F32R)
            aT_hi, aT_lo = sb(ctx, "aT_hi", [P, NG, P], F32R), sb(ctx, "aT_lo", [P, NG, P], F32R)
            st6, mv = sb(ctx, "st6", [P, 6]), sb(ctx, "mv", [P, 2])
            var, rstd = sb(ctx, "var", [P, 1]), sb(ctx, "rstd", [P, 1])
            ssk, ssq = sb(ctx, "ssk", [P, 1]), sb(ctx, "ssq", [P, 1])
            mk, mq = sb(ctx, "mk", [P, 1]), sb(ctx, "mq", [P, 1])
            rk, rq = sb(ctx, "rk", [P, 1]), sb(ctx, "rq", [P, 1])
            nmx = sb(ctx, "nmx", [P, NH])
            rs = sb(ctx, "rs", [P, NH])
            rr = sb(ctx, "rr", [P, NH])

            w_stage = [prob[:, :, :], sb(ctx, "w_stage", [P, KT, D])[:, :, :]]

            ld_w, ld_b = [sem(f"ld_w{n}") for n in range(4)], sem("ld_b")
            ld_x, ld_c, ld_r, st_x2 = ([sem(f"{s}{n}") for n in range(2)] for s in ("ld_x", "ld_c", "ld_r", "st_x2_"))
            wh, wl, cst, kdz, kd_in = sem("weights_hi"), sem("weights_lo"), sem("row_consts"), sem("kd_zero"), sem("kd_in")
            pe_K, pe_Q, pe_Tx, pe_TP, pe_PV, pe_V, pe_Tk, pe_Tq, pe_S, pe_O = (
                sem("pe_" + n) for n in ("K", "Q", "Tx", "TP", "PV", "V", "Tk", "Tq", "S", "O"))
            dv_kb, dv_qb, dv_kf, dv_qf, dv_xT, dv_pT, dv_aT, dv_vb, dv_kT, dv_qT, dv_mx, dv_rr, dv_x2, dv_bs, dv_st, dv_xn = (
                sem("dv_" + n) for n in ("kb", "qb", "kf", "qf", "xT", "pT", "aT", "vb", "kT", "qT", "mx", "rr", "x2", "bs", "st", "xn"))
            ac_sk, ac_sq, ac_xT, ac_pT, ac_aT, ac_v, ac_kT, ac_qT, ac_c, ac_e = (
                sem("ac_" + n) for n in ("sk", "sq", "xT", "pT", "aT", "v", "kT", "qT", "c", "e"))
            po_mk, po_rk, po_mq, po_rq, po_v, po_c, po_r, po_var, po_rs, po_p = (
                sem("po_" + n) for n in ("mk", "rk", "mq", "rq", "v", "c", "r", "var", "rs", "p"))

            BK, BQ, BTX, BTK, BTQ, BV, BO = (bank[n] for n in (4, 5, 6, 5, 7, 5, 6))
            BTP = [bank[n] for n in (7, 4, 6, 4)]

            def has(b):
                return not isinstance(b, int) or 0 <= b < NB

            def first(b):
                return isinstance(b, int) and b == 0

            def run(eng, slot, before=None, after=None):
                if before:
                    before()
                for b in range(3):
                    slot(b, b % 2)
                with eng.Fori(0, (NB - 6) // 2) as i:
                    for j in range(2):
                        slot(i * 2 + (3 + j), (3 + j) % 2)
                for b in range(NB - 3, NB + 1):
                    slot(b, b % 2)
                if after:
                    after()

            def parity_count(b, par):
                return (b - par) // 2 * DMA + DMA if isinstance(b, int) else (b - par) * (DMA // 2) + DMA

            def cols(a, k):
                return a[:, k * P:(k + 1) * P]

            def strip(h):
                return slice(h * HD, (h + 1) * HD)

            block = ctx.enter_context(nc.Block())

            @block.sync
            def _(sp):
                def load(b, par, src, dst, s):
                    sp.dma_start(dst[par][:, :], src[b]).then_inc(s[par], DMA)

                def before():
                    sp.dma_start(ident[:, :], t["ident"]).then_inc(s_const, DMA)
                    for n in range(2):
                        sp.dma_start(gains[:, n:n + 1], t[("g_xattn", "g_ffn")[n]].broadcast_to([P, 1])).then_inc(s_const, DMA)
                    load(0, 0, t["x"], xin, ld_x)
                    load(0, 0, t["ctxT"], cin, ld_c)
                    for n, name in enumerate(("wk", "wq", "wv", "wo")):
                        if n >= 2:
                            sp.wait_ge(wl, n - 1)
                        sp.dma_start(w_stage[n % 2], t[name].rearrange("p (k n) -> p k n", k=KT)).then_inc(ld_w[n], DMA)
                        if n == 1:
                            for dst, src in ((bk, "bk"), (bq, "bq"), (bv, "bv"), (tgbo, "bo"), (nqk, "nq"), (junk_k, "nk")):
                                sp.dma_start(dst[:, :], t[src].broadcast_to([P, D])).then_inc(ld_b, DMA)
                            load(1, 1, t["x"], xin, ld_x)
                            load(1, 1, t["ctxT"], cin, ld_c)
                    sp.wait_ge(dv_xn, 1)
                    load(2, 0, t["x"], xin, ld_x)

                def slot(b, par):
                    if has(b) and has(b + 3):
                        at_least(sp, dv_xn, b + 2, apart=True)
                        load(b + 3, 1 - par, t["x"], xin, ld_x)
                    if has(b) and has(b + 2):
                        at_least(sp, ac_c, b + 1, apart=True)
                        at_least(sp, po_c, b + 1, apart=True)
                        load(b + 2, par, t["ctxT"], cin, ld_c)
                    if has(b):
                        at_least(sp, dv_x2, b - 1, apart=True)
                        load(b, par, t["x"], xres, ld_r)
                        if first(b):
                            sp.wait_ge(kdz, 1)
                        at_least(sp, ac_kT, b + 1, apart=True)
                        at_least(sp, dv_kT, b + 1, apart=True)
                        for h in range(HG):
                            sp.dma_start(kd[strip(h), :, :, h, :].bitcast(F32), kT[strip(h), :, :, :].bitcast(F32)).then_inc(kd_in, DMA)
                    if has(b - 1):
                        at_least(sp, dv_x2, b, apart=True)
                        sp.dma_start(x2_dram[b - 1], x2[1 - par][:, :]).then_inc(st_x2[1 - par], DMA)

                def after():
                    for n in range(2):
                        sp.wait_ge(st_x2[n], NB // 2 * DMA)

                run(sp, slot, before, after)

            @block.tensor
            def _(pe):
                wk, wq, wv, wo = ([(h[:, k, :], l[:, k, :]) for k in range(KT)] for h, l in (W[n] for n in ("wk", "wq", "wv", "wo")))
                cT = [(cols(cT_hi, k), cols(cT_lo, k)) for k in range(KT)]
                xT = [(cols(xnT_hi, k), cols(xnT_lo, k)) for k in range(KT)]

                def turn(src, dst, s):
                    for k in range(KT):
                        mm = pe.transpose(cols(dst, k), cols(src, k), ident[:, :])
                    mm.then_inc(s, 1)

                def turn_x(b):
                    at_least(pe, dv_x2, b - 2)
                    at_least(pe, dv_xn, b + 1)
                    turn(xn, BTX, pe_Tx)

                def turn_probs(a, b, g):
                    if g == 0:
                        at_least(pe, dv_qT, a + 1)
                    if g == 1 and has(b):
                        at_least(pe, dv_kb, b + 1)
                    if g == 2 and has(b + 1):
                        at_least(pe, dv_xT, b + 2)
                    if g == 3:
                        at_least(pe, dv_pT, a * NG + 2)
                    at_least(pe, po_p, a * NG + (g + 1))
                    for h in range(HG):
                        mm = pe.transpose(cols(BTP[g], h), prob[:, g, h * P:(h + 1) * P], ident[:, :])
                    mm.then_inc(pe_TP, 1)

                def values(a, g):
                    if g == 0:
                        at_least(pe, ac_v, a + 1)
                        at_least(pe, po_v, a + 1)
                    at_least(pe, dv_pT, a * NG + (g + 1))
                    mm = mm3(pe, bank[g], [(cols(v_hi, g), cols(v_lo, g))], [(pT_hi[:, g, :], pT_lo[:, g, :])])
                    if g == NG - 1:
                        mm.then_inc(pe_PV, 1)

                def scores(b):
                    at_least(pe, dv_qT, b + 1)
                    at_least(pe, kd_in, (b + 1) * (HG * DMA))
                    for g in range(NG):
                        mm3(pe, bank[g], [(cols(qT_hi, g), cols(qT_lo, g))],
                            [tuple(kd[:, n, g, :, :].rearrange("p h k -> p (h k)") for n in range(2))]).then_inc(pe_S, 1)

                def before():
                    pe.wait_ge(s_const, n_const)
                    turn_x(0)

                def slot(b, par):
                    a = b - 1
                    if has(b):
                        if first(b):
                            pe.wait_ge(wl, 1)
                        at_least(pe, po_c, b + 1)
                        at_least(pe, dv_pT, a * NG)
                        mm3(pe, BK, cT, wk).then_inc(pe_K, 1)
                        if first(b):
                            pe.wait_ge(wl, 2)
                        at_least(pe, dv_vb, b)
                        at_least(pe, dv_xT, b + 1)
                        mm3(pe, BQ, xT, wq).then_inc(pe_Q, 1)
                        if has(b + 1):
                            turn_x(b + 1)
                    if has(a):
                        turn_probs(a, b, 0)
                        turn_probs(a, b, 1)
                        values(a, 0)
                    if has(b):
                        at_least(pe, dv_qb, b + 1)
                        at_least(pe, dv_kf, b + 1)
                        turn(kf, BTK, pe_Tk)
                    if has(a):
                        turn_probs(a, b, 2)
                        values(a, 1)
                    if has(b):
                        at_least(pe, dv_qf, b + 1)
                        turn(qf, BTQ, pe_Tq)
                    if has(a):
                        turn_probs(a, b, 3)
                        values(a, 2)
                        values(a, 3)
                    if has(b):
                        if first(b):
                            pe.wait_ge(wl, 3)
                        at_least(pe, dv_kT, b + 1)
                        mm3(pe, BV, cT, wv).then_inc(pe_V, 1)
                    if has(a):
                        at_least(pe, dv_aT, (a + 1) * HG)
                    if has(b):
                        scores(b)
                    if has(a):
                        if isinstance(a, int) and a == 0:
                            pe.wait_ge(wl, 4)
                        mm3(pe, BO, [(aT_hi[:, g, :], aT_lo[:, g, :]) for g in range(NG)], wo).then_inc(pe_O, 1)

                run(pe, slot, before)

            @block.vector
            def _(dve):
                def sub(dst, a, hi):
                    return dve.tensor_tensor(dst, a, hi.bitcast(F32), ALU.subtract)

                def stats(b, par):
                    at_least(dve, ld_x[par], parity_count(b, par))
                    at_least(dve, po_rs, b)
                    dve.bn_stats(st6[:, :], xin[par][:, :]).then_inc(dv_bs, 1)
                    at_least(dve, dv_xn, b)
                    at_least(dve, dv_bs, b + 1, apart=True)
                    dve.bn_aggr(mv[:, :], st6[:, :]).then_inc(dv_st, 1)

                def normalise(b, par):
                    at_least(dve, po_rs, b + 1)
                    at_least(dve, pe_Tx, b)
                    dve.tensor_scalar(xn[:, :], xin[par][:, :], mv[:, 0:1], rstd[:, 0:1], ALU.subtract, ALU.mult).then_inc(dv_xn, 1)

                def lo_xT(b):
                    at_least(dve, ac_xT, b + 1)
                    sub(xnT_lo[:, :], BTX, xnT_hi[:, :]).then_inc(dv_xT, 1)

                def lo_probs(a, g):
                    at_least(dve, ac_pT, a * NG + (g + 1))
                    sub(pT_lo[:, g, :], BTP[g], pT_hi[:, g, :]).then_inc(dv_pT, 1)

                def maxima(b, g):
                    at_least(dve, pe_S, b * NG + (g + 1))
                    at_least(dve, ac_e, b * NG + (g + 1) - NG)
                    dve.tensor_reduce(nmx[:, g * HG:(g + 1) * HG], bank[g].rearrange("p (h k) -> p h k", h=HG),
                                      AX.X, ALU.max, negate=True).then_inc(dv_mx, 1)

                def inverse(b, g):
                    at_least(dve, ac_e, b * NG + (g + 1))
                    at_least(dve, po_p, b * NG + (g + 1) - NG)
                    hs = slice(g * HG, (g + 1) * HG)
                    dve.reciprocal(rr[:, hs], rs[:, hs]).then_inc(dv_rr, 1)

                def before():
                    stats(0, 0)
                    dve.memset(kd[:, :, :, :, :].bitcast(mybir.dt.uint32), 0).then_inc(kdz, 1)
                    normalise(0, 0)
                    for n, name in enumerate(("wk", "wq", "wv", "wo")):
                        dve.wait_ge(wh, n + 1)
                        sub(W[name][1][:, :, :], w_stage[n % 2], W[name][0][:, :, :]).then_inc(wl, 1)
                        if n == 0:
                            lo_xT(0)
                        if n == 1:
                            dve.wait_ge(ld_b, 6 * DMA)
                            dve.tensor_tensor(nqk[:, :], nqk[:, :], junk_k[:, :], ALU.mult).then_inc(cst, 1)
                            dve.wait_ge(s_tanh, 1)
                            dve.tensor_scalar(tgbo[:, :], tgbo[:, :], tanh_g[:, 0:1], None, ALU.mult).then_inc(cst, 1)
                            stats(1, 1)
                            normalise(1, 1)
                    dve.wait_ge(cst, 2)

                def slot(b, par):
                    a = b - 1
                    if has(a):
                        for g in range(3):
                            inverse(a, g)
                    if has(b):
                        at_least(dve, pe_K, b + 1)
                        dve.tensor_tensor(kb[:, :], BK, bk[:, :], ALU.add).then_inc(dv_kb, 1)
                    if has(a):
                        inverse(a, 3)
                    if has(b):
                        at_least(dve, pe_Q, b + 1)
                        dve.tensor_tensor(qb[:, :], BQ, bq[:, :], ALU.add).then_inc(dv_qb, 1)
                        at_least(dve, po_rk, b + 1)
                        dve.scalar_tensor_tensor(out=kf[:, :], in0=kb[:, :], scalar=rk[:, 0:1], in1=nqk[:, :],
                                                 op0=ALU.mult, op1=ALU.mult).then_inc(dv_kf, 1)
                        if has(b + 1):
                            lo_xT(b + 1)
                    if has(a):
                        lo_probs(a, 0)
                        lo_probs(a, 1)
                    if has(b):
                        at_least(dve, po_rq, b + 1)
                        dve.tensor_scalar(qf[:, :], qb[:, :], rq[:, 0:1], None, ALU.mult).then_inc(dv_qf, 1)
                        at_least(dve, ac_kT, b + 1)
                        sub(kT[:, 1, :, :], BTK.rearrange("p (g k) -> p g k", g=NG), kT[:, 0, :, :]).then_inc(dv_kT, 1)
                    if has(a):
                        lo_probs(a, 2)
                    if has(b):
                        at_least(dve, ac_qT, b + 1)
                        sub(qT_lo[:, :], BTQ, qT_hi[:, :]).then_inc(dv_qT, 1)
                    if has(a):
                        lo_probs(a, 3)
                        for h in range(HG):
                            at_least(dve, ac_aT, a * HG + (h + 1))
                            sub(aT_lo[strip(h), :, :], wide[strip(h), :, h * P:(h + 1) * P], aT_hi[strip(h), :, :]).then_inc(dv_aT, 1)
                    if has(b):
                        at_least(dve, pe_V, b + 1)
                        at_least(dve, po_v, b)
                        dve.tensor_tensor(vb[:, :], BV, bv[:, :], ALU.add).then_inc(dv_vb, 1)
                        for g in range(NG):
                            maxima(b, g)
                    if has(b) and has(b + 2):
                        stats(b + 2, par)
                    if has(a):
                        at_least(dve, po_r, a + 1)
                        if has(a - 2):
                            at_least(dve, st_x2[1 - par], parity_count(a - 2, 1 - par))
                        at_least(dve, pe_O, a + 1)
                        dve.scalar_tensor_tensor(out=x2[1 - par][:, :], in0=BO, scalar=tanh_g[:, 0:1],
                                                 in1=xres[1 - par][:, :], op0=ALU.mult, op1=ALU.add).then_inc(dv_x2, 1)
                    if has(b) and has(b + 2):
                        normalise(b + 2, par)

                run(dve, slot, before)

            @block.scalar
            def _(act):
                def copy(dst, src):
                    return act.activation(dst, src, ACT.Copy)

                def hi_xT(b):
                    at_least(act, pe_Tx, b + 1)
                    copy(xnT_hi[:, :], BTX).then_inc(ac_xT, 1)

                def hi_ctx(b, par):
                    at_least(act, ld_c[par], parity_count(b, par))
                    at_least(act, pe_V, b)
                    copy(cT_hi[:, :], cin[par][:, :]).then_inc(ac_c, 1)

                def hi_probs(a, g):
                    at_least(act, pe_TP, a * NG + (g + 1))
                    copy(pT_hi[:, g, :], BTP[g]).then_inc(ac_pT, 1)

                def exps(b, g):
                    at_least(act, dv_mx, b * NG + (g + 1))
                    at_least(act, dv_rr, b * NG + (g + 1) - NG)
                    for h in range(HG):
                        n = g * HG + h
                        i = act.activation(prob[:, g, h * P:(h + 1) * P], cols(bank[g], h), ACT.Exp,
                                           bias=nmx[:, n:n + 1], scale=1.0, accum_out=rs[:, n:n + 1])
                    i.then_inc(ac_e, 1)

                def before():
                    act.wait_ge(s_const, n_const)
                    act.activation(tanh_g[:, :], gains[:, :], ACT.Tanh).then_inc(s_tanh, 1)
                    hi_ctx(0, 0)
                    for n, name in enumerate(("wk", "wq", "wv", "wo")):
                        act.wait_ge(ld_w[n], DMA)
                        copy(W[name][0][:, :, :], w_stage[n % 2]).then_inc(wh, 1)
                        if n == 0:
                            hi_xT(0)
                    act.wait_ge(wl, 4)
                    act.wait_ge(cst, 2)

                def slot(b, par):
                    a = b - 1
                    if has(b):
                        at_least(act, dv_kb, b + 1)
                        at_least(act, po_mk, b)
                        act.activation(junk_k[:, :], kb[:, :], ACT.Square, accum_out=ssk[:, :]).then_inc(ac_sk, 1)
                        if has(b + 1):
                            hi_xT(b + 1)
                        at_least(act, dv_qb, b + 1)
                        at_least(act, po_mq, b)
                        act.activation(junk_q[:, :], qb[:, :], ACT.Square, accum_out=ssq[:, :]).then_inc(ac_sq, 1)
                    if has(a):
                        hi_probs(a, 0)
                        hi_probs(a, 1)
                    if has(b):
                        at_least(act, pe_Tk, b + 1)
                        at_least(act, kd_in, b * (HG * DMA))
                        copy(kT[:, 0, :, :], BTK.rearrange("p (g k) -> p g k", g=NG)).then_inc(ac_kT, 1)
                    if has(a):
                        hi_probs(a, 2)
                    if has(b):
                        at_least(act, pe_Tq, b + 1)
                        copy(qT_hi[:, :], BTQ).then_inc(ac_qT, 1)
                    if has(a):
                        hi_probs(a, 3)
                        at_least(act, pe_PV, a + 1)
                        for h in range(HG):
                            copy(aT_hi[strip(h), :, :], wide[strip(h), :, h * P:(h + 1) * P]).then_inc(ac_aT, 1)
                    if has(b):
                        at_least(act, dv_vb, b + 1)
                        copy(v_hi[:, :], vb[:, :]).then_inc(ac_v, 1)
                        for g in range(NG):
                            exps(b, g)
                            if g == 0 and has(b + 1):
                                hi_ctx(b + 1, 1 - par)

                run(act, slot, before)

            @block.gpsimd
            def _(pool):
                def power(r, m, got, count, s):
                    at_least(pool, got, count)
                    pool.tensor_tensor(r[:, :], m[:, :], powers[:, 0:1], ALU.pow).then_inc(s, 1)

                def inv_rms(b, ss, m, r, got, s_m, s_r, scale):
                    at_least(pool, got, b + 1, apart=True)
                    pool.tensor_scalar(m[:, :], ss[:, :], scale / D, scale * EPS_RMS, ALU.mult, ALU.add).then_inc(s_m, 1)
                    power(r, m, s_m, b + 1, s_r)

                def lo_ctx(b, par):
                    at_least(pool, ac_c, b + 1)
                    pool.tensor_tensor(cT_lo[:, :], cin[par][:, :], cT_hi[:, :].bitcast(F32), ALU.subtract).then_inc(po_c, 1)

                def inv_std(b):
                    at_least(pool, dv_xn, b)
                    at_least(pool, dv_st, b + 1, apart=True)
                    pool.tensor_scalar(var[:, :], mv[:, 1:2], EPS_LN, None, ALU.add).then_inc(po_var, 1)
                    power(rstd, var, po_var, b + 1, po_rs)

                def divide(b, g):
                    at_least(pool, dv_rr, b * NG + (g + 1))
                    p = prob[:, g, :].rearrange("p (h k) -> p h k", h=HG)
                    r = rr[:, g * HG:(g + 1) * HG].unsqueeze(2).broadcast_to([P, HG, P])
                    pool.tensor_tensor(p, p, r, ALU.mult).then_inc(po_p, 1)

                def before():
                    pool.memset(powers[:, :], -0.5).then_inc(s_pow, 1)
                    pool.wait_ge(s_pow, 1)
                    inv_std(0)
                    lo_ctx(0, 0)
                    inv_std(1)

                def slot(b, par):
                    a = b - 1
                    if has(a):
                        for g in range(3):
                            divide(a, g)
                    if has(b):
                        inv_rms(b, ssk, mk, rk, ac_sk, po_mk, po_rk, 1.0)
                    if has(a):
                        divide(a, 3)
                    if has(b):
                        inv_rms(b, ssq, mq, rq, ac_sq, po_mq, po_rq, float(HD))
                        if first(b):
                            pool.wait_ge(cst, 2)
                        at_least(pool, ld_r[par], parity_count(b, par))
                        pool.tensor_tensor(xres[par][:, :], xres[par][:, :], tgbo[:, :], ALU.add).then_inc(po_r, 1)
                        at_least(pool, ac_v, b + 1)
                        pool.tensor_tensor(v_lo[:, :], vb[:, :], v_hi[:, :].bitcast(F32), ALU.subtract).then_inc(po_v, 1)
                        if has(b + 1):
                            lo_ctx(b + 1, 1 - par)
                        if has(b + 2):
                            inv_std(b + 2)

                run(pool, slot, before)

            del block

        with ExitStack() as ctx:
            feed_forward(nc, ctx, t, out, x2_dram, bank, ident, tanh_g, powers, s_const, n_const, at_least, mm3)


def feed_forward(nc, ctx, t, out, x2_dram, bank, ident, tanh_g, powers, s_const, n_const, at_least, mm3):
    NB = t["x"].shape[0]
    NI = t["down"].shape[1] // D
    NE = t["gate"].shape[1] // KT
    GB = D // P
    NGRP = NB // GB

    def sb(name, shape, dt=F32):
        return ctx.enter_context(nc.sbuf_tensor(name, shape, dt))

    def sem(name):
        return ctx.enter_context(nc.semaphore(name))

    up_hi, up_lo = sb("up_hi", [P, NI, KT * P], F32R), sb("up_lo", [P, NI, KT * P], F32R)
    dn_hi, dn_lo = sb("dn_hi", [P, NI, D], F32R), sb("dn_lo", [P, NI, D], F32R)
    ex_hi, ex_lo = sb("ex_hi", [P, KT, D], F32R), sb("ex_lo", [P, KT, D], F32R)
    ga_hi, ga_lo = sb("ga_hi", [P, KT * NE], F32R), sb("ga_lo", [P, KT * NE], F32R)
    ga_raw = sb("ga_raw", [P, KT * NE])
    xT_hi, xT_lo = sb("fxT_hi", [P, KT, D], F32R), sb("fxT_lo", [P, KT, D], F32R)
    hT_hi = [sb(f"hT_hi{n}", [P, D], F32R) for n in range(2)]
    hT_lo = [sb(f"hT_lo{n}", [P, D], F32R) for n in range(2)]
    relu, hid = sb("relu", [P, D]), sb("hid", [P, D])
    xin = [sb(f"fxin{n}", [P, D]) for n in range(2)]
    xn = [sb(f"fxn{n}", [P, D]) for n in range(2)]
    moe = [sb(f"moe{n}", [P, D]) for n in range(2)]
    y = [sb(f"y{n}", [P, D]) for n in range(GB)]
    res = [sb(f"fres{n}", [P, D]) for n in range(2)]
    gamma, beta = sb("gamma", [P, D]), sb("beta", [P, D])
    lg = sb("lg", [NE, D])
    top, route = sb("top", [P, GB, 8]), sb("route", [P, GB])
    st6, mv, var, rstd = sb("fst6", [P, 6]), sb("fmv", [P, 2]), sb("fvar", [P, 1]), sb("frstd", [P, 1])
    yvar = sb("yvar", [P, GB])
    yst6, ymv, yrstd = sb("yst6", [P, GB, 6]), sb("ymv", [P, GB, 2]), sb("yrstd", [P, GB])
    nstage = 4
    stage = y

    ld_s = [sem(f"ld_s{n}") for n in range(nstage)]
    fh, fl, fcst, ld_g = sem("f_hi"), sem("f_lo"), sem("f_consts"), sem("ld_g")
    ld_x, ld_r, st_o = ([sem(f"f{s}{n}") for n in range(2)] for s in ("ld_x", "ld_r", "st_o"))
    pe_T, pe_G, pe_TG, pe_U, pe_D, pe_E = (sem("fpe_" + n) for n in ("T", "G", "TG", "U", "D", "E"))
    ac_T, ac_G, ac_r, ac_h, ac_m = (sem("fac_" + n) for n in ("T", "G", "r", "h", "m"))
    dv_T, dv_bs, dv_st, dv_top, dv_s, dv_h, dv_l, dv_y, dv_yb, dv_ys, dv_a, dv_o = (
        sem("fdv_" + n) for n in ("T", "bs", "st", "top", "s", "h", "l", "y", "yb", "ys", "a", "o"))
    po_var, po_rs, po_xn, po_r, po_yv, po_ys = (sem("fpo_" + n) for n in ("var", "rs", "xn", "r", "yv", "ys"))

    def run(eng, group, before=None, after=None):
        if before:
            before()
        group(0)
        with eng.Fori(1, NGRP - 1) as i:
            group(i)
        group(NGRP - 1)
        if after:
            after()

    def static(g):
        return isinstance(g, int)

    def half(n, c):
        return n * (GB // 2 * DMA) + (c // 2 + 1) * DMA

    pieces = [(t["up"].rearrange("p (i n) -> p i n", i=NI)[:, i, :], up_hi[:, i, :], up_lo[:, i, :]) for i in range(NI)]
    pieces += [(t["down"].rearrange("p (i n) -> p i n", i=NI)[:, i, :], dn_hi[:, i, :], dn_lo[:, i, :]) for i in range(NI)]
    order = [n for i in range(NI) for n in (i, NI + i)]
    pieces = [pieces[n] for n in order]
    pieces += [(t["ex"].rearrange("p (k n) -> p k n", k=KT)[:, k, :], ex_hi[:, k, :], ex_lo[:, k, :]) for k in range(KT)]

    block = ctx.enter_context(nc.Block())

    @block.sync
    def _(sp):
        def load_x(g, j):
            sp.dma_start(xin[j % 2][:, :], x2_dram[g * GB + j]).then_inc(ld_x[j % 2], DMA)

        def before():
            for src, dst in (("gamma", gamma), ("beta", beta)):
                sp.dma_start(dst[:, :], t[src].broadcast_to([P, D])).then_inc(ld_g, DMA)
            sp.dma_start(ga_raw[:, :], t["gate"]).then_inc(ld_g, DMA)
            for n in range(2):
                sp.sem_inc(st_o[n], DMA)
            load_x(0, 0)
            load_x(0, 1)
            for n, (src, _, _) in enumerate(pieces):
                sp.wait_ge(fl, n - nstage + 2) if n >= nstage else None
                sp.dma_start(stage[n % nstage][:, :], src).then_inc(ld_s[n % nstage], DMA)
                if n == 1:
                    for j in (2, 3):
                        sp.wait_ge(po_xn, j - 1)
                        load_x(0, j)

        def group(g):
            last = static(g) and g == NGRP - 1
            for j in range(GB):
                if j == 2 and not (static(g) and g == 0):
                    finish(g - 1)
                if not last:
                    at_least(sp, po_xn, g * GB + (GB + j - 1), apart=True)
                    load_x(g + 1, j)

        def finish(g):
            for j in range(GB):
                sp_res(g, j)
                at_least(sp, dv_o, g * GB + (j + 1), apart=True)
                sp.dma_start(out[g * GB + j], res[j % 2][:, :]).then_inc(st_o[j % 2], DMA)

        def sp_res(g, j):
            at_least(sp, st_o[j % 2], half(g, j), apart=True)
            sp.dma_start(res[j % 2][:, :], x2_dram[g * GB + j]).then_inc(ld_r[j % 2], DMA)

        def after():
            finish(NGRP - 1)
            for n in range(2):
                sp.wait_ge(st_o[n], (NB // 2 + 1) * DMA)

        run(sp, group, before, after)

    @block.tensor
    def _(pe):
        def turn(g, j):
            at_least(pe, po_xn, g * GB + (j + 1))
            if not (static(g) and g == 0 and j == 0):
                if j:
                    at_least(pe, ac_T, g * GB + j)
                    at_least(pe, dv_T, g * GB + j)
                else:
                    at_least(pe, dv_top, g)
            for k in range(KT):
                mm = pe.transpose(bank[7][:, k * P:(k + 1) * P], xn[j % 2][:, k * P:(k + 1) * P], ident[:, :])
            mm.then_inc(pe_T, 1)

        def upward(g, i):
            if static(g) and g == 0:
                pe.wait_ge(fl, 2 * i + 2)
            if i < 2:
                at_least(pe, ac_r, g * NI + (i - 1))
            else:
                at_least(pe, ac_r, g * NI + (i - 1))
            mm3(pe, bank[4 + i % 2],
                [(up_hi[:, i, k * P:(k + 1) * P], up_lo[:, i, k * P:(k + 1) * P]) for k in range(KT)],
                [(xT_hi[:, k, :], xT_lo[:, k, :]) for k in range(KT)]).then_inc(pe_U, 1)

        def downward(g, i):
            if static(g) and g == 0:
                pe.wait_ge(fl, 2 * i + 3)
            at_least(pe, dv_l, g * NI + (i + 1))
            for j in range(GB):
                c = slice(j * P, (j + 1) * P)
                if i == 0:
                    at_least(pe, dv_y, (g - 1) * GB + (j + 1))
                mm = mm3(pe, bank[j], [(hT_hi[i % 2][:, c], hT_lo[i % 2][:, c])],
                         [(dn_hi[:, i, :], dn_lo[:, i, :])], first=i == 0, last=i == NI - 1)
            mm.then_inc(pe_D, 1)

        def expert(g, j):
            if static(g) and g == 0 and j == 0:
                pe.wait_ge(fl, len(pieces) + 1)
            c = slice(j * P, (j + 1) * P)
            if j == 0:
                at_least(pe, ac_G, g + 1)
            else:
                at_least(pe, ac_m, g * GB + j)
            mm3(pe, bank[6], [(xT_hi[:, k, c], xT_lo[:, k, c]) for k in range(KT)],
                [(ex_hi[:, k, :], ex_lo[:, k, :]) for k in range(KT)]).then_inc(pe_E, 1)

        def before():
            for j in range(GB):
                turn(0, j)

        def group(g):
            last = static(g) and g == NGRP - 1
            at_least(pe, ac_T, g * GB + GB)
            at_least(pe, dv_T, g * GB + GB)
            at_least(pe, ac_m, g * GB)
            if static(g) and g == 0:
                pe.wait_ge(fl, 1)
            mm3(pe, bank[6][0:NE, :], [(ga_hi[:, k * NE:(k + 1) * NE], ga_lo[:, k * NE:(k + 1) * NE]) for k in range(KT)],
                [(xT_hi[:, k, :], xT_lo[:, k, :]) for k in range(KT)]).then_inc(pe_G, 1)
            upward(g, 0)
            at_least(pe, ac_G, g + 1, apart=True)
            for j in range(GB):
                mm = pe.transpose(bank[7][:, j * NE:(j + 1) * NE], lg[0:NE, j * P:(j + 1) * P], ident[0:NE, 0:NE])
            mm.then_inc(pe_TG, 1)
            for i in range(1, NI):
                upward(g, i)
                downward(g, i - 1)
            expert(g, 0)
            if not last:
                turn(g + 1, 0)
            downward(g, NI - 1)
            for j in range(1, GB):
                expert(g, j)
                if not last:
                    turn(g + 1, j)

        run(pe, group, before)

    @block.scalar
    def _(act):
        def copy(dst, src):
            return act.activation(dst, src, ACT.Copy)

        def hi_T(g, j):
            at_least(act, pe_T, g * GB + (j + 1))
            copy(xT_hi[:, :, j * P:(j + 1) * P], bank[7].rearrange("p (k n) -> p k n", k=KT)).then_inc(ac_T, 1)

        def before():
            act.wait_ge(ld_g, 3 * DMA)
            copy(ga_hi[:, :], ga_raw[:, :]).then_inc(fh, 1)
            for n, (_, hi, _) in enumerate(pieces):
                act.wait_ge(ld_s[n % nstage], (n // nstage + 1) * DMA)
                copy(hi, stage[n % nstage][:, :]).then_inc(fh, 1)
                if n < GB:
                    hi_T(0, n)

        def tile_hi(g, i):
            at_least(act, pe_U, g * NI + (i + 1))
            at_least(act, dv_h, g * NI + i)
            act.activation(relu[:, :], bank[4 + i % 2], ACT.Relu).then_inc(ac_r, 1)
            at_least(act, dv_h, g * NI + (i + 1))
            at_least(act, pe_D, g * NI + (i - 1))
            copy(hT_hi[i % 2][:, :], hid[:, :]).then_inc(ac_h, 1)

        def weigh(g, j):
            at_least(act, dv_s, g + 1)
            at_least(act, pe_E, g * GB + (j + 1))
            at_least(act, dv_y, g * GB + (j - 1))
            act.activation(moe[j % 2][:, :], bank[6], ACT.Copy, scale=route[:, j:j + 1]).then_inc(ac_m, 1)

        def group(g):
            last = static(g) and g == NGRP - 1
            at_least(act, pe_G, g + 1)
            copy(lg[:, :], bank[6][0:NE, :]).then_inc(ac_G, 1)
            for i in range(NI):
                tile_hi(g, i)
            for j in range(GB):
                weigh(g, j)
                if not last:
                    hi_T(g + 1, j)

        run(act, group, before)

    @block.vector
    def _(dve):
        def stats(g, j):
            at_least(dve, ld_x[j % 2], half(g, j))
            at_least(dve, po_xn, g * GB + j)
            dve.bn_stats(st6[:, :], xin[j % 2][:, :]).then_inc(dv_bs, 1)
            at_least(dve, dv_bs, g * GB + (j + 1), apart=True)
            dve.bn_aggr(mv[:, :], st6[:, :]).then_inc(dv_st, 1)

        def lo_T(g, j):
            c = slice(j * P, (j + 1) * P)
            at_least(dve, ac_T, g * GB + (j + 1))
            dve.tensor_tensor(xT_lo[:, :, c], bank[7].rearrange("p (k n) -> p k n", k=KT),
                              xT_hi[:, :, c].bitcast(F32), ALU.subtract).then_inc(dv_T, 1)

        def before():
            stats(0, 0)
            stats(0, 1)
            dve.wait_ge(ld_g, 3 * DMA)
            dve.tensor_scalar(gamma[:, :], gamma[:, :], tanh_g[:, 1:2], None, ALU.mult).then_inc(fcst, 1)
            dve.tensor_scalar(beta[:, :], beta[:, :], tanh_g[:, 1:2], None, ALU.mult).then_inc(fcst, 1)
            dve.wait_ge(fh, 1)
            dve.tensor_tensor(ga_lo[:, :], ga_raw[:, :], ga_hi[:, :].bitcast(F32), ALU.subtract).then_inc(fl, 1)
            for n, (_, hi, lo) in enumerate(pieces):
                dve.wait_ge(fh, n + 2)
                dve.tensor_tensor(lo, stage[n % nstage][:, :], hi.bitcast(F32), ALU.subtract).then_inc(fl, 1)
                if n < GB:
                    lo_T(0, n)
                    if n < 2:
                        stats(0, 2 + n)
            dve.wait_ge(fcst, 2)
            dve.wait_ge(fl, len(pieces) + 1)

        def hidden(g, i):
            at_least(dve, ac_h, g * NI + i)
            at_least(dve, dv_l, g * NI + i)
            at_least(dve, ac_r, g * NI + (i + 1))
            dve.tensor_tensor(hid[:, :], relu[:, :], relu[:, :], ALU.mult).then_inc(dv_h, 1)
            at_least(dve, ac_h, g * NI + (i + 1))
            dve.tensor_tensor(hT_lo[i % 2][:, :], hid[:, :], hT_hi[i % 2][:, :].bitcast(F32), ALU.subtract).then_inc(dv_l, 1)

        def routing(g):
            at_least(dve, pe_TG, g + 1)
            at_least(dve, ac_m, g * GB, apart=True)
            for j in range(GB):
                i = dve.max(top[:, j, :], bank[7][:, j * NE:(j + 1) * NE])
            i.then_inc(dv_top, 1)
            at_least(dve, dv_top, g + 1)
            dve.tensor_tensor(route[:, :], top[:, :, 0], top[:, :, 1], ALU.add).then_inc(dv_s, 1)

        def add(g, j):
            at_least(dve, pe_D, g * NI + NI)
            at_least(dve, ac_m, g * GB + (j + 1))
            dve.tensor_tensor(y[j][:, :], bank[j], moe[j % 2][:, :], ALU.add).then_inc(dv_y, 1)

        def y_stats(g, j):
            at_least(dve, dv_y, g * GB + (j + 1))
            dve.bn_stats(yst6[:, j, :], y[j][:, :]).then_inc(dv_yb, 1)
            at_least(dve, dv_yb, g * GB + (j + 1), apart=True)
            dve.bn_aggr(ymv[:, j, :], yst6[:, j, :]).then_inc(dv_ys, 1)

        def result(g, j):
            at_least(dve, dv_ys, g * GB + (j + 1))
            dve.scalar_tensor_tensor(out=y[j][:, :], in0=y[j][:, :], scalar=ymv[:, j, 0:1], in1=gamma[:, :],
                                     op0=ALU.subtract, op1=ALU.mult).then_inc(dv_a, 1)
            at_least(dve, dv_a, g * GB + (j + 1))
            at_least(dve, po_ys, g * GB + (j + 1))
            at_least(dve, po_r, g * GB + (j + 1))
            dve.scalar_tensor_tensor(out=res[j % 2][:, :], in0=y[j][:, :], scalar=yrstd[:, j:j + 1], in1=res[j % 2][:, :],
                                     op0=ALU.mult, op1=ALU.add).then_inc(dv_o, 1)

        def group(g):
            last = static(g) and g == NGRP - 1
            for i in range(NI):
                hidden(g, i)
                if i == 0:
                    routing(g)
                if not (static(g) and g == 0):
                    if 1 <= i <= GB:
                        y_stats(g - 1, i - 1)
                    if 2 <= i <= GB + 1:
                        result(g - 1, i - 2)
                if not last and i >= 8 and i % 2 == 0 and (i - 8) // 2 < GB:
                    stats(g + 1, (i - 8) // 2)
            if not last:
                lo_T(g + 1, 0)
            add(g, 0)
            for j in range(1, GB):
                if not last:
                    lo_T(g + 1, j)
                add(g, j)

        def after():
            for j in range(GB):
                y_stats(NGRP - 1, j)
                result(NGRP - 1, j)

        run(dve, group, before, after)

    @block.gpsimd
    def _(pool):
        def normalise(g, j):
            at_least(pool, dv_st, g * GB + (j + 1), apart=True)
            pool.tensor_scalar(var[:, :], mv[:, 1:2], EPS_LN, None, ALU.add).then_inc(po_var, 1)
            at_least(pool, po_var, g * GB + (j + 1))
            pool.tensor_tensor(rstd[:, :], var[:, :], powers[:, 0:1], ALU.pow).then_inc(po_rs, 1)
            at_least(pool, pe_T, g * GB + (j - 1))
            at_least(pool, po_rs, g * GB + (j + 1), apart=True)
            pool.tensor_scalar(xn[j % 2][:, :], xin[j % 2][:, :], mv[:, 0:1], rstd[:, 0:1], ALU.subtract, ALU.mult).then_inc(po_xn, 1)

        def scale_y(g, j):
            at_least(pool, dv_ys, g * GB + (j + 1), apart=True)
            pool.tensor_scalar(yvar[:, j:j + 1], ymv[:, j, 1:2], EPS_LN, None, ALU.add).then_inc(po_yv, 1)
            at_least(pool, po_yv, g * GB + (j + 1))
            pool.tensor_tensor(yrstd[:, j:j + 1], yvar[:, j:j + 1], powers[:, 0:1], ALU.pow).then_inc(po_ys, 1)

        def residual(g, j):
            at_least(pool, ld_r[j % 2], half(g, j))
            pool.tensor_tensor(res[j % 2][:, :], res[j % 2][:, :], beta[:, :], ALU.add).then_inc(po_r, 1)

        def before():
            for j in range(GB):
                normalise(0, j)
            pool.wait_ge(fcst, 2)

        def group(g):
            last = static(g) and g == NGRP - 1
            if not (static(g) and g == 0):
                finish(g - 1)
            if not last:
                for j in range(GB):
                    normalise(g + 1, j)

        def finish(g):
            for j in range(GB):
                residual(g, j)
                scale_y(g, j)

        def after():
            finish(NGRP - 1)

        run(pool, group, before, after)


def kernel(**inputs):
    import numpy as np
    import concourse.bacc as bacc
    from concourse.bass_utils import run_bass_kernel_spmd

    def f(name):
        return np.asarray(inputs[name])

    def rows_on_partitions(w):
        return np.ascontiguousarray(w.reshape(-1, P, w.shape[1]).transpose(1, 0, 2).reshape(P, -1))

    ctxt = f("ctx_2048")
    nb = ctxt.shape[0]
    up = f("L0_ffn_up_w")
    arrays = {
        "x": f("x"),
        "ctxT": ctxt.transpose(0, 2, 1).reshape(nb, KT, P, P).transpose(0, 2, 1, 3).reshape(nb, P, KT * P),
        "ident": np.eye(P, dtype=np.float32),
        "g_xattn": f("g_xattn").reshape(1, 1),
        "g_ffn": f("g_ffn").reshape(1, 1),
        "wq": rows_on_partitions(f("L0_xattn_q_w").T),
        "wk": rows_on_partitions(f("L0_xattn_k_img_w").T),
        "wv": rows_on_partitions(f("L0_xattn_v_img_w").T),
        "wo": rows_on_partitions(f("L0_xattn_o_w").T),
        "bq": f("L0_xattn_q_b").reshape(1, D),
        "bk": f("L0_xattn_k_img_b").reshape(1, D),
        "bv": f("L0_xattn_v_img_b").reshape(1, D),
        "bo": f("L0_xattn_o_b").reshape(1, D),
        "nq": f("L0_xattn_norm_q_w").reshape(1, D),
        "nk": f("L0_xattn_norm_k_img_w").reshape(1, D),
        "gate": rows_on_partitions(f("L0_ffn_gate_w")),
        "up": up.reshape(KT, P, -1, P).transpose(1, 2, 0, 3).reshape(P, -1),
        "down": rows_on_partitions(f("L0_ffn_down_w")),
        "ex": rows_on_partitions(f("L0_ffn_expert_weight")),
        "gamma": f("L0_ffn_ln_gamma").reshape(1, D),
        "beta": f("L0_ffn_ln_beta").reshape(1, D),
    }
    arrays = {n: np.ascontiguousarray(a) for n, a in arrays.items()}
    nc = bacc.Bacc("TRN2", target_bir_lowering=False, num_devices=1)
    t = {n: nc.dram_tensor("in_" + n, a.shape, mybir.dt.from_np(a.dtype), kind="ExternalInput").ap() for n, a in arrays.items()}
    out = nc.dram_tensor("out_x", arrays["x"].shape, F32, kind="ExternalOutput").ap()
    flamingo_layer(nc, t, out)
    r = run_bass_kernel_spmd(nc, [{"in_" + n: a for n, a in arrays.items()}], core_ids=[0])
    return r.results[0]["out_x"]
```

```python
from contextlib import ExitStack

import concourse.bass as bass
from concourse import mybir

F32 = mybir.dt.float32
F32R = mybir.dt.float32r
ALU = mybir.AluOpType
ACT = mybir.ActivationFunctionType
AX = mybir.AxisListType

P = 128
D = 512
KT = D // P
NH = 16
HD = D // NH
HG = P // HD
NG = NH // HG
EPS_LN = 1e-5
EPS_RMS = 1e-6
DMA = 16


def flamingo_layer(nc, t, out):
    NB = t["x"].shape[0]
    GB = D // P

    x2_dram = nc.dram_tensor("x2_scratch", [NB, P, D], F32, kind="Internal").ap()

    def at_least(eng, sem, value, apart=False):
        if isinstance(value, int) and value <= 0:
            return
        eng.wait_ge(sem, value)
        if apart and not isinstance(value, int):
            eng.sem_inc(passed[eng], 1)

    with ExitStack() as whole:
        def sem(name):
            return whole.enter_context(nc.semaphore(name))

        def sb(ctx, name, shape, dt=F32):
            return ctx.enter_context(nc.sbuf_tensor(name, shape, dt))

        wide = whole.enter_context(nc.psum_tensor("wide", [P, NG, D], F32))
        bank = [wide[:, n, :] for n in range(NG)]
        bank += [whole.enter_context(nc.psum_tensor(f"bank{n}", [P, D], F32))[:, :] for n in range(NG, 8)]
        ident = sb(whole, "ident", [P, P])
        gains = sb(whole, "gains", [P, 2])
        tanh_g = sb(whole, "tanh_g", [P, 2])
        powers = sb(whole, "powers", [P, 1])

        s_ident, s_gains = sem("ident_loaded"), sem("gains_loaded")
        passed = {e: sem(f"passed_{n}") for n, e in enumerate((nc.sync, nc.tensor, nc.vector, nc.gpsimd))}
        s_tanh = sem("tanh_done")
        s_pow = sem("powers_set")

        def mm3(eng, dst, stat, mov, first=True, last=True, ready=None):
            n = len(stat)
            for k, ((ah, al), (bh, bl)) in enumerate(zip(stat, mov)):
                if ready:
                    ready(k)
                eng.matmul(dst, ah, bh, start=first and k == 0, stop=False)
                eng.matmul(dst, ah, bl, start=False, stop=False)
                mm = eng.matmul(dst, al, bh, start=False, stop=last and k == n - 1)
            return mm

        WN = ("wk", "wq", "wv", "wo")
        W = {n: (sb(whole, n + "_hi", [P, KT, D], F32R), sb(whole, n + "_lo", [P, KT, D], F32R)) for n in WN}
        fx = sb(whole, "fx", [P, GB, D])
        fy = sb(whole, "fy", [P, GB, D])
        st_x2 = [sem(f"st_x2_{n}") for n in range(2)]
        dv_x2, pe_V = sem("dv_x2"), sem("pe_V")
        ff = feed_forward_start(nc, whole, t, x2_dram, bank, ident, tanh_g, powers, W, fx, fy, at_least, mm3)

        block = whole.enter_context(nc.Block())

        with ExitStack() as ctx:
            bk = sb(ctx, "bk", [P, D])
            bq = sb(ctx, "bq", [P, D])
            bv = sb(ctx, "bv", [P, D])
            tgbo = sb(ctx, "tgbo", [P, D])
            nqk = sb(ctx, "nqk", [P, D])
            xin = [sb(ctx, f"xin{n}", [P, D]) for n in range(2)]
            cin = [sb(ctx, f"cin{n}", [P, D]) for n in range(2)]
            xres = [sb(ctx, f"xres{n}", [P, D]) for n in range(2)]
            x2 = [sb(ctx, f"x2_{n}", [P, D]) for n in range(2)]
            xn = sb(ctx, "xn", [P, D])
            xnT_hi, xnT_lo = sb(ctx, "xnT_hi", [P, D], F32R), sb(ctx, "xnT_lo", [P, D], F32R)
            cT_hi, cT_lo = sb(ctx, "cT_hi", [P, D], F32R), sb(ctx, "cT_lo", [P, D], F32R)
            kb, qb, vb = sb(ctx, "kb", [P, D]), sb(ctx, "qb", [P, D]), sb(ctx, "vb", [P, D])
            kf, qf = sb(ctx, "kf", [P, D]), sb(ctx, "qf", [P, D])
            junk_k, junk_q = sb(ctx, "junk_k", [P, D]), sb(ctx, "junk_q", [P, D])
            v_hi, v_lo = sb(ctx, "v_hi", [P, D], F32R), sb(ctx, "v_lo", [P, D], F32R)
            qT_hi, qT_lo = sb(ctx, "qT_hi", [P, D], F32R), sb(ctx, "qT_lo", [P, D], F32R)
            kT = sb(ctx, "kT", [P, 2, NG, P], F32R)
            kd = sb(ctx, "kd", [P, 2, NG, HG, P], F32R)
            prob = sb(ctx, "prob", [P, NG, HG * P])
            pT_hi, pT_lo = sb(ctx, "pT_hi", [P, NG, HG * P], F32R), sb(ctx, "pT_lo", [P, NG, HG * P], F32R)
            aT = sb(ctx, "aT", [P, NG, P])
            aT_hi, aT_lo = sb(ctx, "aT_hi", [P, NG, P], F32R), sb(ctx, "aT_lo", [P, NG, P], F32R)
            st6, mv = sb(ctx, "st6", [P, 6]), sb(ctx, "mv", [P, 2])
            var, rstd = sb(ctx, "var", [P, 1]), sb(ctx, "rstd", [P, 1])
            ssk, ssq = sb(ctx, "ssk", [P, 1]), sb(ctx, "ssq", [P, 1])
            mk, mq = sb(ctx, "mk", [P, 1]), sb(ctx, "mq", [P, 1])
            rk, rq = sb(ctx, "rk", [P, 1]), sb(ctx, "rq", [P, 1])
            nmx = sb(ctx, "nmx", [P, NH])
            rs = sb(ctx, "rs", [P, NH])
            rr = sb(ctx, "rr", [P, NH])

            w_stage = [prob, fx, fy, fx]

            ld_w = [[sem(f"ld_w{n}{k}") for k in range(KT)] for n in range(4)]
            ld_bk, ld_bq, ld_bv, ld_bo, ld_n = (sem("ld_" + n) for n in ("bk", "bq", "bv", "bo", "norms"))
            ld_x, ld_c, ld_r = ([sem(f"{s}{n}") for n in range(2)] for s in ("ld_x", "ld_c", "ld_r"))
            wh, wl, cst, kdz, kd_in = sem("weights_hi"), sem("weights_lo"), sem("row_consts"), sem("kd_zero"), sem("kd_in")
            pe_K, pe_Q, pe_Tx, pe_TP, pe_PV, pe_Tk, pe_Tq, pe_S, pe_O = (
                sem("pe_" + n) for n in ("K", "Q", "Tx", "TP", "PV", "Tk", "Tq", "S", "O"))
            dv_kb, dv_qb, dv_kf, dv_qf, dv_xT, dv_pT, dv_ah, dv_aT, dv_vb, dv_kT, dv_qT, dv_mx, dv_rr, dv_bs, dv_st, dv_xn = (
                sem("dv_" + n) for n in ("kb", "qb", "kf", "qf", "xT", "pT", "ah", "aT", "vb", "kT", "qT", "mx", "rr", "bs", "st", "xn"))
            ac_sk, ac_sq, ac_xT, ac_pT, ac_aT, ac_v, ac_kT, ac_qT, ac_c, ac_e = (
                sem("ac_" + n) for n in ("sk", "sq", "xT", "pT", "aT", "v", "kT", "qT", "c", "e"))
            po_mk, po_rk, po_mq, po_rq, po_v, po_c, po_r, po_var, po_rs, po_p = (
                sem("po_" + n) for n in ("mk", "rk", "mq", "rq", "v", "c", "r", "var", "rs", "p"))

            BK, BQ, BTK, BTX, BTQ, BV, BO = (bank[n] for n in (4, 7, 6, 7, 4, 5, 6))
            BTP = [bank[n] for n in (5, 6, 4, 5)]

            def has(b):
                return not isinstance(b, int) or 0 <= b < NB

            def ff_pair(b):
                return (b - (NB - 2)) * 2 if isinstance(b, int) and NB - 2 <= b < NB else None

            def is_slot(b, n):
                return isinstance(b, int) and b == n

            def first(b):
                return isinstance(b, int) and b == 0

            def run(eng, slot, before=None):
                if before:
                    before()
                for b in range(3):
                    slot(b, b % 2)
                with eng.Fori(0, (NB - 6) // 2) as i:
                    for j in range(2):
                        slot(i * 2 + (3 + j), (3 + j) % 2)
                for b in range(NB - 3, NB + 1):
                    slot(b, b % 2)

            def parity_count(b, par):
                return (b - par) // 2 * DMA + DMA if isinstance(b, int) else (b - par) * (DMA // 2) + DMA

            def cols(a, k):
                return a[:, k * P:(k + 1) * P]

            def strip(h):
                return slice(h * HD, (h + 1) * HD)

            @block.sync
            def _(sp):
                def weight(n):
                    w = t[WN[n]].rearrange("p (k n) -> p k n", k=KT)
                    for k in range(KT):
                        sp.dma_start(w_stage[n][:, k, :], w[:, k, :]).then_inc(ld_w[n][k], DMA)

                def row(dst, src, s):
                    sp.dma_start(dst[:, :], t[src].broadcast_to([P, D])).then_inc(s, DMA)

                def load(b, par, src, dst, s):
                    sp.dma_start(dst[par][:, :], src[b]).then_inc(s[par], DMA)

                def before():
                    load(0, 0, t["x"], xin, ld_x)
                    sp.dma_start(ident[:, :], t["ident"]).then_inc(s_ident, DMA)
                    load(0, 0, t["ctxT"], cin, ld_c)
                    weight(0)
                    row(bk, "bk", ld_bk)
                    weight(1)
                    row(nqk, "nq", ld_n)
                    row(junk_q, "nk", ld_n)
                    row(bq, "bq", ld_bq)
                    load(1, 1, t["x"], xin, ld_x)
                    weight(2)
                    row(bv, "bv", ld_bv)
                    load(1, 1, t["ctxT"], cin, ld_c)

                def before_second():
                    for n in range(2):
                        sp.dma_start(gains[:, n:n + 1], t[("g_xattn", "g_ffn")[n]].broadcast_to([P, 1])).then_inc(s_gains, DMA)
                    row(tgbo, "bo", ld_bo)
                    sp.wait_ge(wl, 2 * KT)
                    weight(3)
                    sp.wait_ge(dv_xn, 1)
                    load(2, 0, t["x"], xin, ld_x)

                def slot(b, par):
                    if has(b) and has(b + 2):
                        at_least(sp, ac_c, b + 1, apart=True)
                        at_least(sp, po_c, b + 1, apart=True)
                        load(b + 2, par, t["ctxT"], cin, ld_c)
                    if has(b):
                        at_least(sp, dv_x2, b - 1, apart=True)
                        load(b, par, t["x"], xres, ld_r)
                        if first(b):
                            sp.wait_ge(kdz, 2)
                        at_least(sp, ac_kT, b + 1, apart=True)
                        at_least(sp, dv_kT, b + 1, apart=True)
                        for h in range(HG):
                            sp.dma_start(kd[strip(h), :, :, h, :].bitcast(F32), kT[strip(h), :, :, :].bitcast(F32)).then_inc(kd_in, DMA)
                        if first(b):
                            before_second()
                    if has(b) and has(b + 3):
                        at_least(sp, dv_xn, b + 2, apart=True)
                        load(b + 3, 1 - par, t["x"], xin, ld_x)
                    if is_slot(b, NB):
                        for n in range(ff.nstage, 2 * ff.nstage):
                            ff.load_piece(sp, n)
                    if has(b - 1):
                        at_least(sp, dv_x2, b, apart=True)
                        sp.dma_start(x2_dram[b - 1], x2[1 - par][:, :]).then_inc(st_x2[1 - par], DMA)
                    if is_slot(b, NB - 3):
                        for n in range(2):
                            sp.wait_ge(st_x2[n], GB // 2 * DMA)
                        ff.load_first(sp)

                run(sp, slot, before)

            @block.tensor
            def _(pe):
                wk, wq, wv, wo = ([(h[:, k, :], l[:, k, :]) for k in range(KT)] for h, l in (W[n] for n in WN))
                cT = [(cols(cT_hi, k), cols(cT_lo, k)) for k in range(KT)]
                xT = [(cols(xnT_hi, k), cols(xnT_lo, k)) for k in range(KT)]

                def split_weight(b, n):
                    return (lambda k: pe.wait_ge(wl, n * KT + k + 1)) if first(b) else None

                def turn(src, dst, s):
                    for k in range(KT):
                        mm = pe.transpose(cols(dst, k), cols(src, k), ident[:, :])
                    mm.then_inc(s, 1)

                def turn_x(b):
                    if has(b - 1):
                        at_least(pe, dv_qb, b)
                    at_least(pe, dv_xn, b + 1)
                    turn(xn, BTX, pe_Tx)

                def turn_probs(a, b, g):
                    if g == 0:
                        at_least(pe, dv_vb, a + 1)
                    if g == 1:
                        at_least(pe, dv_x2, a)
                    if g == 2 and has(b):
                        at_least(pe, dv_kb, b + 1)
                    if g == 3:
                        at_least(pe, dv_pT, a * NG + 1)
                    at_least(pe, po_p, a * NG + (g + 1))
                    for h in range(HG):
                        mm = pe.transpose(cols(BTP[g], h), prob[:, g, h * P:(h + 1) * P], ident[:, :])
                    mm.then_inc(pe_TP, 1)

                def values(a, g):
                    if g == 0:
                        at_least(pe, ac_v, a + 1)
                        at_least(pe, po_v, a + 1)
                    at_least(pe, dv_pT, a * NG + (g + 1))
                    mm = mm3(pe, bank[g], [(cols(v_hi, g), cols(v_lo, g))], [(pT_hi[:, g, :], pT_lo[:, g, :])])
                    if g == NG - 1:
                        mm.then_inc(pe_PV, 1)

                def scores(b):
                    at_least(pe, dv_qT, b + 1)
                    at_least(pe, kd_in, (b + 1) * (HG * DMA))
                    for g in range(NG):
                        mm3(pe, bank[g], [(cols(qT_hi, g), cols(qT_lo, g))],
                            [tuple(kd[:, n, g, :, :].rearrange("p h k -> p (h k)") for n in range(2))]).then_inc(pe_S, 1)

                def before():
                    pe.wait_ge(s_ident, DMA)
                    turn_x(0)

                def slot(b, par):
                    a = b - 1
                    b_last = is_slot(b, NB)
                    if has(b):
                        at_least(pe, po_c, b + 1)
                        at_least(pe, dv_qT, b)
                        mm3(pe, BK, cT, wk, ready=split_weight(b, 0)).then_inc(pe_K, 1)
                    if b_last:
                        ff.turn(pe, 0, 0)
                    if has(a):
                        turn_probs(a, b, 0)
                        turn_probs(a, b, 1)
                    if b_last:
                        ff.turn(pe, 0, 1)
                    if has(b):
                        at_least(pe, dv_xT, b + 1)
                        mm3(pe, BQ, xT, wq, ready=split_weight(b, 1)).then_inc(pe_Q, 1)
                    if has(a):
                        turn_probs(a, b, 2)
                    if has(b):
                        at_least(pe, dv_kf, b + 1)
                        turn(kf, BTK, pe_Tk)
                    if has(a):
                        values(a, 0)
                        turn_probs(a, b, 3)
                        if b_last:
                            ff.turn(pe, 0, 2)
                        values(a, 1)
                        values(a, 2)
                        if b_last:
                            ff.turn(pe, 0, 3)
                    if has(b + 1) and not first(b):
                        turn_x(b + 1)
                    if has(a):
                        values(a, 3)
                    if b_last:
                        pe.wait_ge(dv_pT, a * NG + 3)
                        ff.upward(pe, 0, 0)
                    if has(b):
                        at_least(pe, dv_qf, b + 1)
                        turn(qf, BTQ, pe_Tq)
                        mm3(pe, BV, cT, wv, ready=split_weight(b, 2)).then_inc(pe_V, 1)
                    if has(a):
                        at_least(pe, ac_aT, a + 1)
                    if has(b):
                        scores(b)
                    if first(b):
                        turn_x(1)
                    if has(a):
                        if first(a):
                            pe.wait_ge(wl, 4 * KT)
                        at_least(pe, dv_aT, a + 1)
                        at_least(pe, dv_kT, b + 1 if has(b) else b)
                        mm3(pe, BO, [(aT_hi[:, g, :], aT_lo[:, g, :]) for g in range(NG)], wo).then_inc(pe_O, 1)

                run(pe, slot, before)

            @block.vector
            def _(dve):
                def sub(dst, a, hi):
                    return dve.tensor_tensor(dst, a, hi.bitcast(F32), ALU.subtract)

                def stats(b, par):
                    at_least(dve, ld_x[par], parity_count(b, par))
                    at_least(dve, po_rs, b)
                    dve.bn_stats(st6[:, :], xin[par][:, :]).then_inc(dv_bs, 1)
                    at_least(dve, dv_xn, b)
                    at_least(dve, dv_bs, b + 1, apart=True)
                    dve.bn_aggr(mv[:, :], st6[:, :]).then_inc(dv_st, 1)

                def normalise(b, par):
                    at_least(dve, po_rs, b + 1)
                    at_least(dve, pe_Tx, b)
                    dve.tensor_scalar(xn[:, :], xin[par][:, :], mv[:, 0:1], rstd[:, 0:1], ALU.subtract, ALU.mult).then_inc(dv_xn, 1)

                def lo_xT(b):
                    at_least(dve, ac_xT, b + 1)
                    sub(xnT_lo[:, :], BTX, xnT_hi[:, :]).then_inc(dv_xT, 1)

                def lo_probs(a, g):
                    at_least(dve, ac_pT, a * NG + (g + 1))
                    sub(pT_lo[:, g, :], BTP[g], pT_hi[:, g, :]).then_inc(dv_pT, 1)

                def maxima(b, g):
                    at_least(dve, pe_S, b * NG + (g + 1))
                    at_least(dve, ac_e, b * NG + (g + 1) - NG)
                    dve.tensor_reduce(nmx[:, g * HG:(g + 1) * HG], bank[g].rearrange("p (h k) -> p h k", h=HG),
                                      AX.X, ALU.max, negate=True).then_inc(dv_mx, 1)

                def inverse(b, g):
                    at_least(dve, ac_e, b * NG + (g + 1))
                    at_least(dve, po_p, b * NG + (g + 1) - NG)
                    hs = slice(g * HG, (g + 1) * HG)
                    dve.reciprocal(rr[:, hs], rs[:, hs]).then_inc(dv_rr, 1)

                def weight_lo(n, k):
                    hi, lo = W[WN[n]]
                    dve.wait_ge(wh, n * KT + k + 1)
                    sub(lo[:, k, :], w_stage[n][:, k, :], hi[:, k, :]).then_inc(wl, 1)

                def before():
                    dve.memset(kd[:, 0, :, :, :].bitcast(mybir.dt.uint32), 0).then_inc(kdz, 1)
                    stats(0, 0)
                    normalise(0, 0)
                    weight_lo(0, 0)
                    lo_xT(0)
                    for k in range(1, KT):
                        weight_lo(0, k)
                    for k in range(KT):
                        weight_lo(1, k)

                def slot(b, par):
                    a = b - 1
                    b_last = is_slot(b, NB)
                    if has(b):
                        if first(b):
                            dve.wait_ge(ld_bk, DMA)
                        at_least(dve, pe_K, b + 1)
                        dve.tensor_tensor(kb[:, :], BK, bk[:, :], ALU.add).then_inc(dv_kb, 1)
                    if has(a):
                        inverse(a, 3)
                        if first(a):
                            weight_lo(3, 0)
                        if b_last:
                            ff.lo_T(dve, 0, 0)
                        lo_probs(a, 0)
                        if first(a):
                            weight_lo(3, 1)
                        lo_probs(a, 1)
                    if b_last:
                        ff.normalise(dve, 0, 3)
                        ff.lo_T(dve, 0, 1)
                    if has(b):
                        if first(b):
                            dve.wait_ge(ld_n, 2 * DMA)
                            dve.tensor_tensor(nqk[:, :], nqk[:, :], junk_q[:, :], ALU.mult).then_inc(cst, 1)
                            dve.wait_ge(cst, 1)
                            dve.wait_ge(ld_bq, DMA)
                        at_least(dve, po_rk, b + 1)
                        dve.scalar_tensor_tensor(out=kf[:, :], in0=kb[:, :], scalar=rk[:, 0:1], in1=nqk[:, :],
                                                 op0=ALU.mult, op1=ALU.mult).then_inc(dv_kf, 1)
                        if ff_pair(b - 1) is not None:
                            ff.normalise(dve, 0, ff_pair(b - 1) + 1)
                        at_least(dve, pe_Q, b + 1)
                        dve.tensor_tensor(qb[:, :], BQ, bq[:, :], ALU.add).then_inc(dv_qb, 1)
                    if has(a):
                        if first(a):
                            weight_lo(3, 2)
                        lo_probs(a, 2)
                    if b_last:
                        ff.piece_lo(dve, 0)
                    if has(b):
                        at_least(dve, ac_kT, b + 1)
                        sub(kT[:, 1, :, :], BTK.rearrange("p (g k) -> p g k", g=NG), kT[:, 0, :, :]).then_inc(dv_kT, 1)
                    if has(a):
                        lo_probs(a, 3)
                        if first(a):
                            weight_lo(3, 3)
                    if b_last:
                        ff.lo_T(dve, 0, 2)
                        ff.lo_T(dve, 0, 3)
                    if has(b):
                        at_least(dve, po_rq, b + 1)
                        dve.tensor_scalar(qf[:, :], qb[:, :], rq[:, 0:1], None, ALU.mult).then_inc(dv_qf, 1)
                    if first(b):
                        for k in range(KT):
                            weight_lo(2, k)
                        stats(1, 1)
                    if has(b + 1) and not first(b):
                        lo_xT(b + 1)
                    if has(b):
                        at_least(dve, ac_qT, b + 1)
                        sub(qT_lo[:, :], BTQ, qT_hi[:, :]).then_inc(dv_qT, 1)
                        normalise(1, 1) if first(b) else None
                    if has(a):
                        at_least(dve, ac_aT, a + 1)
                        at_least(dve, pe_O, a)
                        dve.tensor_scalar(aT_hi[:, :, :], aT[:, :, :], 0.0, None, ALU.add).then_inc(dv_ah, 1)
                        at_least(dve, dv_ah, a + 1)
                        sub(aT_lo[:, :, :], aT[:, :, :], aT_hi[:, :, :]).then_inc(dv_aT, 1)
                    if b_last:
                        ff.prepare(dve)
                    if has(b):
                        if first(b):
                            dve.wait_ge(ld_bv, DMA)
                        at_least(dve, pe_V, b + 1)
                        at_least(dve, po_v, b)
                        dve.tensor_tensor(vb[:, :], BV, bv[:, :], ALU.add).then_inc(dv_vb, 1)
                        if first(b):
                            dve.wait_ge(ld_bo, DMA)
                            dve.wait_ge(s_tanh, 1)
                            dve.tensor_scalar(tgbo[:, :], tgbo[:, :], tanh_g[:, 0:1], None, ALU.mult).then_inc(cst, 1)
                        for g in range(NG):
                            maxima(b, g)
                        inverse(b, 0)
                        lo_xT(1) if first(b) else None
                        if has(b + 2):
                            stats(b + 2, par)
                        if ff_pair(b) is not None:
                            ff.stats(dve, 0, ff_pair(b))
                        inverse(b, 1)
                    if has(a):
                        at_least(dve, po_r, a + 1)
                        if has(a - 2):
                            at_least(dve, st_x2[1 - par], parity_count(a - 2, 1 - par))
                        at_least(dve, pe_O, a + 1)
                        dve.scalar_tensor_tensor(out=x2[1 - par][:, :], in0=BO, scalar=tanh_g[:, 0:1],
                                                 in1=xres[1 - par][:, :], op0=ALU.mult, op1=ALU.add).then_inc(dv_x2, 1)
                    if has(b):
                        inverse(b, 2)
                        if has(b + 2):
                            normalise(b + 2, par)
                        if ff_pair(b) is not None:
                            ff.normalise(dve, 0, ff_pair(b))
                            ff.stats(dve, 0, ff_pair(b) + 1)

                run(dve, slot, before)

            @block.scalar
            def _(act):
                def copy(dst, src):
                    return act.activation(dst, src, ACT.Copy)

                def hi_xT(b):
                    at_least(act, pe_Tx, b + 1)
                    copy(xnT_hi[:, :], BTX).then_inc(ac_xT, 1)

                def hi_ctx(b, par):
                    at_least(act, ld_c[par], parity_count(b, par))
                    at_least(act, pe_V, b)
                    copy(cT_hi[:, :], cin[par][:, :]).then_inc(ac_c, 1)

                def hi_probs(a, g):
                    at_least(act, pe_TP, a * NG + (g + 1))
                    copy(pT_hi[:, g, :], BTP[g]).then_inc(ac_pT, 1)

                def exps(b, g):
                    at_least(act, dv_mx, b * NG + (g + 1))
                    at_least(act, dv_rr, b * NG + (g + 1) - NG)
                    for h in range(HG):
                        n = g * HG + h
                        i = act.activation(prob[:, g, h * P:(h + 1) * P], cols(bank[g], h), ACT.Exp,
                                           bias=nmx[:, n:n + 1], scale=1.0, accum_out=rs[:, n:n + 1])
                    i.then_inc(ac_e, 1)

                def weight_hi(n, k):
                    act.wait_ge(ld_w[n][k], DMA)
                    copy(W[WN[n]][0][:, k, :], w_stage[n][:, k, :]).then_inc(wh, 1)

                def before():
                    hi_ctx(0, 0)
                    weight_hi(0, 0)
                    hi_xT(0)
                    for k in range(1, KT):
                        weight_hi(0, k)
                    for k in range(KT):
                        weight_hi(1, k)

                def slot(b, par):
                    a = b - 1
                    b_last = is_slot(b, NB)
                    if b_last:
                        ff.hi_T(act, 0, 0)
                    if has(a):
                        hi_probs(a, 0)
                    if has(b):
                        at_least(act, dv_kb, b + 1)
                        at_least(act, po_mk, b)
                        act.activation(junk_k[:, :], kb[:, :], ACT.Square, accum_out=ssk[:, :]).then_inc(ac_sk, 1)
                    if has(a):
                        hi_probs(a, 1)
                        if b_last:
                            ff.hi_T(act, 0, 1)
                        hi_probs(a, 2)
                    if b_last:
                        act.wait_ge(pe_V, NB)
                        ff.piece_hi(act, 0)
                    if has(b):
                        at_least(act, pe_Tk, b + 1)
                        at_least(act, kd_in, b * (HG * DMA))
                        copy(kT[:, 0, :, :], BTK.rearrange("p (g k) -> p g k", g=NG)).then_inc(ac_kT, 1)
                        if first(b):
                            act.wait_ge(cst, 1)
                        at_least(act, dv_qb, b + 1)
                        at_least(act, po_mq, b)
                        act.activation(junk_q[:, :], qb[:, :], ACT.Square, accum_out=ssq[:, :]).then_inc(ac_sq, 1)
                    if first(b):
                        for k in range(KT):
                            weight_hi(2, k)
                    if has(a):
                        hi_probs(a, 3)
                    if b_last:
                        ff.hi_T(act, 0, 2)
                        ff.hi_T(act, 0, 3)
                    if has(b + 1) and not first(b):
                        hi_xT(b + 1)
                    if has(a):
                        at_least(act, pe_PV, a + 1)
                        at_least(act, dv_aT, a)
                    for h in range(HG):
                        if h == 2 and has(b):
                            at_least(act, pe_Tq, b + 1)
                            copy(qT_hi[:, :], BTQ).then_inc(ac_qT, 1)
                        if has(a):
                            i = copy(aT[strip(h), :, :], wide[strip(h), :, h * P:(h + 1) * P])
                    if has(a):
                        i.then_inc(ac_aT, 1)
                    if has(b + 1):
                        hi_ctx(b + 1, 1 - par)
                    if first(b):
                        act.wait_ge(s_gains, 2 * DMA)
                        act.activation(tanh_g[:, :], gains[:, :], ACT.Tanh).then_inc(s_tanh, 1)
                        act.wait_ge(wl, KT)
                    if has(b):
                        for g in range(NG):
                            exps(b, g)
                            if g == 0:
                                at_least(act, dv_vb, b + 1)
                                copy(v_hi[:, :], vb[:, :]).then_inc(ac_v, 1)
                                hi_xT(1) if first(b) else None
                    if first(b):
                        for k in range(KT):
                            weight_hi(3, k)

                run(act, slot, before)

            @block.gpsimd
            def _(pool):
                def power(r, m, got, count, s):
                    at_least(pool, got, count)
                    pool.tensor_tensor(r[:, :], m[:, :], powers[:, 0:1], ALU.pow).then_inc(s, 1)

                def inv_rms(b, ss, m, r, got, s_m, s_r, scale):
                    at_least(pool, got, b + 1, apart=True)
                    pool.tensor_scalar(m[:, :], ss[:, :], scale / D, scale * EPS_RMS, ALU.mult, ALU.add).then_inc(s_m, 1)
                    power(r, m, s_m, b + 1, s_r)

                def lo_ctx(b, par):
                    at_least(pool, ac_c, b + 1)
                    pool.tensor_tensor(cT_lo[:, :], cin[par][:, :], cT_hi[:, :].bitcast(F32), ALU.subtract).then_inc(po_c, 1)

                def inv_std(b):
                    at_least(pool, dv_xn, b)
                    at_least(pool, dv_st, b + 1, apart=True)
                    pool.tensor_scalar(var[:, :], mv[:, 1:2], EPS_LN, None, ALU.add).then_inc(po_var, 1)
                    power(rstd, var, po_var, b + 1, po_rs)

                def divide(b, g):
                    at_least(pool, dv_rr, b * NG + (g + 1))
                    p = prob[:, g, :].rearrange("p (h k) -> p h k", h=HG)
                    r = rr[:, g * HG:(g + 1) * HG].unsqueeze(2).broadcast_to([P, HG, P])
                    pool.tensor_tensor(p, p, r, ALU.mult).then_inc(po_p, 1)

                def before():
                    pool.memset(powers[:, :], -0.5).then_inc(s_pow, 1)
                    pool.memset(kd[:, 1, :, :, :].bitcast(mybir.dt.uint32), 0).then_inc(kdz, 1)
                    pool.wait_ge(s_pow, 1)
                    inv_std(0)
                    lo_ctx(0, 0)

                def slot(b, par):
                    a = b - 1
                    if has(b):
                        inv_rms(b, ssk, mk, rk, ac_sk, po_mk, po_rk, 1.0)
                    if has(a):
                        divide(a, 3)
                    if has(b):
                        inv_rms(b, ssq, mq, rq, ac_sq, po_mq, po_rq, float(HD))
                        if first(b):
                            inv_std(1)
                            lo_ctx(1, 1)
                            pool.wait_ge(cst, 2)
                        at_least(pool, ld_r[par], parity_count(b, par))
                        pool.tensor_tensor(xres[par][:, :], xres[par][:, :], tgbo[:, :], ALU.add).then_inc(po_r, 1)
                        if has(b + 1) and not first(b):
                            lo_ctx(b + 1, 1 - par)
                        at_least(pool, ac_v, b + 1)
                        pool.tensor_tensor(v_lo[:, :], vb[:, :], v_hi[:, :].bitcast(F32), ALU.subtract).then_inc(po_v, 1)
                        divide(b, 0)
                        if has(b + 2):
                            inv_std(b + 2)
                        if ff_pair(b) is not None:
                            ff.inv_std(pool, 0, ff_pair(b))
                        divide(b, 1)
                        divide(b, 2)
                        if ff_pair(b) is not None:
                            ff.inv_std(pool, 0, ff_pair(b) + 1)

                run(pool, slot, before)

        with ExitStack() as ctx:
            feed_forward(nc, ctx, block, ff, t, out, x2_dram, bank, ident, tanh_g, powers, dv_x2, st_x2, at_least, mm3)


def feed_forward_start(nc, whole, t, x2_dram, bank, ident, tanh_g, powers, W, fx, fy, at_least, mm3):
    NB = t["x"].shape[0]
    NI = t["down"].shape[1] // D
    NE = t["gate"].shape[1] // KT
    GB = D // P

    def sb(name, shape, dt=F32):
        return whole.enter_context(nc.sbuf_tensor(name, shape, dt))

    def sem(name):
        return whole.enter_context(nc.semaphore(name))

    gamma, beta = sb("gamma", [P, D]), sb("beta", [P, D])
    ga = sb("ga", [P, KT, 2, NE], F32R)
    ga_hi, ga_lo = ga[:, :, 0, :], ga[:, :, 1, :]
    ga_raw = sb("ga_raw", [P, KT, NE])
    two_ident = sb("two_ident", [2 * NE, NE])
    hT_hi = [sb(f"hT_hi{n}", [P, D], F32R) for n in range(2)]
    hT_lo = [sb(f"hT_lo{n}", [P, D], F32R) for n in range(2)]
    relu, hid, lg = sb("relu", [P, D]), sb("hid", [P, D]), sb("lg", [2 * NE, D])
    st6, mv, var, rstd = sb("fst6", [P, 6]), sb("fmv", [P, 2]), sb("fvar", [P, 1]), sb("frstd", [P, 1])
    xT_hi, xT_lo = W["wk"]
    ex_hi, ex_lo = W["wo"]
    up = [(W["wq"][0][:, n, :], W["wq"][1][:, n, :]) for n in range(KT)]
    down = [(W["wv"][0][:, n, :], W["wv"][1][:, n, :]) for n in range(KT)]
    xn = [fx[:, n, :] for n in range(GB)]
    y = [fy[:, n, :] for n in range(GB)]
    nstage = GB
    stage = y
    BG, BTG = bank[6], bank[7]
    BE = [bank[n] for n in (6, 4, 6, 4)]

    ld_s = [sem(f"ld_s{n}") for n in range(nstage)]
    fh, fl, fcst, ld_g, ga_split = (sem("f_" + n) for n in ("hi", "lo", "consts", "ld_g", "ga_split"))
    ld_x = [sem(f"fld_x{n}") for n in range(GB)]
    ld_r, st_o = ([sem(f"f{s}{n}") for n in range(GB)] for s in ("ld_r", "st_o"))
    pe_T, pe_G, pe_TG, pe_U, pe_D, pe_E = (sem("fpe_" + n) for n in ("T", "G", "TG", "U", "D", "E"))
    ac_T, ac_G, ac_r, ac_h, ac_m = (sem("fac_" + n) for n in ("T", "G", "r", "h", "m"))
    dv_T, dv_bs, dv_st, dv_xn, dv_top, dv_s, dv_h, dv_l, dv_y, dv_yb, dv_ys, dv_a, dv_o = (
        sem("fdv_" + n) for n in ("T", "bs", "st", "xn", "top", "s", "h", "l", "y", "yb", "ys", "a", "o"))
    po_var, po_rs, po_r, po_yv, po_ys = (sem("fpo_" + n) for n in ("var", "rs", "r", "yv", "ys"))

    pieces = []
    place = {}

    def piece(kind, n):
        place[kind, n] = len(pieces)
        tiles = KT if kind == "ex" else NI
        pieces.append((t[kind].rearrange("p (i n) -> p i n", i=tiles)[:, n, :], kind, n))

    for i in range(NI):
        piece("up", i)
        piece("down", i)
        if NI - KT - 2 <= i < NI - 2:
            piece("ex", i - (NI - KT - 2))

    def parts(n):
        _, kind, i = pieces[n]
        return (ex_hi[:, i, :], ex_lo[:, i, :]) if kind == "ex" else {"up": up, "down": down}[kind][i]

    def have(kind, n):
        return place[kind, n] + 1

    def load_x(sp, g, j):
        sp.dma_start(xn[j], x2_dram[g * GB + j]).then_inc(ld_x[j], DMA)

    def load_piece(sp, n):
        if n >= nstage:
            sp.wait_ge(fl, n - nstage + 1)
        sp.dma_start(stage[n % nstage], pieces[n][0]).then_inc(ld_s[n % nstage], DMA)

    def load_first(sp):
        for j in range(GB):
            load_x(sp, 0, j)
        for n in range(nstage):
            load_piece(sp, n)
        sp.dma_start(ga_raw[:, :, :], t["gate"].rearrange("p (k n) -> p k n", k=KT)).then_inc(ld_g, DMA)
        sp.dma_start(two_ident[:, :], t["two_ident"]).then_inc(ld_g, DMA)
        for src, dst in (("gamma", gamma), ("beta", beta)):
            sp.dma_start(dst[:, :], t[src].broadcast_to([P, D])).then_inc(ld_g, DMA)

    def turn(pe, g, j):
        at_least(pe, dv_xn, g * GB + (j + 1))
        if isinstance(g, int) and g == 0:
            dst = bank[7]
            at_least(pe, dv_T, j)
        else:
            dst = bank[7 - j % 2 * 2]
            if j >= 2:
                at_least(pe, dv_T, g * GB + (j - 1))
            elif j == 1:
                at_least(pe, ac_r, g * NI)
        for k in range(KT):
            mm = pe.transpose(dst[:, k * P:(k + 1) * P], xn[j][:, k * P:(k + 1) * P], ident[:, :])
        mm.then_inc(pe_T, 1)

    def turned(g, j):
        b = bank[7] if isinstance(g, int) and g == 0 else bank[7 - j % 2 * 2]
        return b.rearrange("p (k n) -> p k n", k=KT)

    def upward(pe, g, i):
        if isinstance(g, int) and g == 0:
            pe.wait_ge(fl, have("up", i))
        if i == 0:
            at_least(pe, ac_T, g * GB + GB)
            at_least(pe, dv_T, g * GB + GB)
            at_least(pe, ac_m, g * GB)
        elif i > 1:
            at_least(pe, ac_r, g * NI + (i - 1))
        mm3(pe, bank[4 + i % 2], [tuple(w[:, k * P:(k + 1) * P] for w in up[i]) for k in range(KT)],
            [(xT_hi[:, k, :], xT_lo[:, k, :]) for k in range(KT)]).then_inc(pe_U, 1)

    def hi_T(act, g, j):
        at_least(act, pe_T, g * GB + (j + 1))
        act.activation(xT_hi[:, :, j * P:(j + 1) * P], turned(g, j), ACT.Copy).then_inc(ac_T, 1)

    def piece_hi(act, n):
        act.wait_ge(ld_s[n % nstage], (n // nstage + 1) * DMA)
        act.activation(parts(n)[0], stage[n % nstage], ACT.Copy).then_inc(fh, 1)

    def stats(dve, g, j):
        at_least(dve, ld_x[j], g * DMA + DMA)
        dve.bn_stats(st6[:, :], xn[j]).then_inc(dv_bs, 1)
        at_least(dve, po_rs, g * GB + j)
        at_least(dve, dv_xn, g * GB + j)
        at_least(dve, dv_bs, g * GB + (j + 1), apart=True)
        dve.bn_aggr(mv[:, :], st6[:, :]).then_inc(dv_st, 1)

    def normalise(dve, g, j):
        at_least(dve, po_rs, g * GB + (j + 1))
        dve.tensor_scalar(xn[j], xn[j], mv[:, 0:1], rstd[:, 0:1], ALU.subtract, ALU.mult).then_inc(dv_xn, 1)

    def lo_T(dve, g, j):
        c = slice(j * P, (j + 1) * P)
        at_least(dve, ac_T, g * GB + (j + 1))
        dve.tensor_tensor(xT_lo[:, :, c], turned(g, j), xT_hi[:, :, c].bitcast(F32), ALU.subtract).then_inc(dv_T, 1)

    def piece_lo(dve, n):
        hi, lo = parts(n)
        dve.wait_ge(fh, n + 1)
        dve.tensor_tensor(lo, stage[n % nstage], hi.bitcast(F32), ALU.subtract).then_inc(fl, 1)

    def prepare(dve):
        dve.wait_ge(ld_g, 4 * DMA)
        dve.tensor_scalar(gamma[:, :], gamma[:, :], tanh_g[:, 1:2], None, ALU.mult).then_inc(fcst, 1)
        dve.tensor_scalar(beta[:, :], beta[:, :], tanh_g[:, 1:2], None, ALU.mult).then_inc(fcst, 1)
        dve.wait_ge(ga_split, 1)
        dve.tensor_tensor(ga_lo, ga_raw[:, :, :], ga_hi.bitcast(F32), ALU.subtract).then_inc(fcst, 1)
        for n in range(1, nstage):
            piece_lo(dve, n)
        dve.wait_ge(fcst, 2)

    def inv_std(pool, g, j):
        at_least(pool, dv_xn, g * GB + j)
        at_least(pool, dv_st, g * GB + (j + 1), apart=True)
        pool.tensor_scalar(var[:, :], mv[:, 1:2], EPS_LN, None, ALU.add).then_inc(po_var, 1)
        at_least(pool, po_var, g * GB + (j + 1))
        pool.tensor_tensor(rstd[:, :], var[:, :], powers[:, 0:1], ALU.pow).then_inc(po_rs, 1)

    class start:
        pass

    start.GB, start.NB, start.NE, start.NI = (
        GB, NB, NE, NI)
    start.ac_G, start.ac_h, start.ac_m, start.ac_r, start.dv_a, start.dv_h, start.dv_l, start.dv_o = (
        ac_G, ac_h, ac_m, ac_r, dv_a, dv_h, dv_l, dv_o)
    start.dv_s, start.dv_top, start.dv_y, start.dv_yb, start.dv_ys, start.fcst, start.fl, start.ga_split = (
        dv_s, dv_top, dv_y, dv_yb, dv_ys, fcst, fl, ga_split)
    start.ld_g, start.ld_r, start.pe_D, start.pe_E, start.pe_G, start.pe_T, start.pe_TG, start.pe_U = (
        ld_g, ld_r, pe_D, pe_E, pe_G, pe_T, pe_TG, pe_U)
    start.po_r, start.po_ys, start.po_yv, start.st_o = (
        po_r, po_ys, po_yv, st_o)
    start.BE, start.BG, start.BTG, start.beta, start.down, start.ex_hi, start.ex_lo, start.ga_hi = (
        BE, BG, BTG, beta, down, ex_hi, ex_lo, ga_hi)
    start.ga_lo, start.ga_raw, start.gamma, start.hT_hi, start.hT_lo, start.have, start.hi_T, start.hid = (
        ga_lo, ga_raw, gamma, hT_hi, hT_lo, have, hi_T, hid)
    start.inv_std, start.lg, start.lo_T, start.load_first, start.load_piece, start.load_x, start.normalise, start.nstage = (
        inv_std, lg, lo_T, load_first, load_piece, load_x, normalise, nstage)
    start.piece_hi, start.piece_lo, start.pieces, start.place, start.prepare, start.relu, start.stats, start.turn = (
        piece_hi, piece_lo, pieces, place, prepare, relu, stats, turn)
    start.up, start.upward, start.xT_hi, start.xT_lo, start.y = (
        up, upward, xT_hi, xT_lo, y)
    start.ga, start.two_ident = ga, two_ident
    return start


def feed_forward(nc, ctx, block, ff, t, out, x2_dram, bank, ident, tanh_g, powers, dv_x2, st_x2, at_least, mm3):
    NB, NI, NE, GB = ff.NB, ff.NI, ff.NE, ff.GB
    NGRP = NB // GB

    def sb(name, shape, dt=F32):
        return ctx.enter_context(nc.sbuf_tensor(name, shape, dt))

    for name, w in (("up", ff.up), ("down", ff.down)):
        hi, lo = (sb(f"{name}_{part}", [P, NI - KT, D], F32R) for part in ("hi", "lo"))
        w += [(hi[:, n, :], lo[:, n, :]) for n in range(NI - KT)]
    res = [sb(f"fres{n}", [P, D]) for n in range(GB)]
    top, route = sb("top", [P, GB, 8]), sb("route", [P, GB])
    yvar = sb("yvar", [P, GB])
    yst6, ymv, yrstd = sb("yst6", [P, GB, 6]), sb("ymv", [P, GB, 2]), sb("yrstd", [P, GB])

    def run(eng, group, before=None, after=None):
        if before:
            before()
        group(0)
        with eng.Fori(1, NGRP - 1) as i:
            group(i)
        group(NGRP - 1)
        if after:
            after()

    def static(g):
        return isinstance(g, int)

    def due(i):
        end = ff.place["up", i + 3] if i + 3 < NI else len(ff.pieces)
        return range(ff.place["up", i + 2], end) if i + 2 < NI else range(0)

    first_new = ff.place["up", KT]

    def freed(eng):
        eng.wait_ge(dv_x2, NB)
        for n in range(2):
            eng.wait_ge(st_x2[n], NB // 2 * DMA)

    @block.sync
    def _(sp):
        def before():
            for n in range(GB):
                sp.sem_inc(ff.st_o[n], DMA)
            for n in range(2 * ff.nstage, len(ff.pieces)):
                ff.load_piece(sp, n)
                if n < 2 * ff.nstage + GB:
                    next_x(0, n - 2 * ff.nstage)
            freed(sp)

        def next_x(g, j):
            at_least(sp, ff.pe_T, g * GB + (j + 1), apart=True)
            ff.load_x(sp, g + 1, j)

        def group(g):
            first, last = (static(g) and g == n for n in (0, NGRP - 1))
            for j in range(GB):
                if not first and not last:
                    next_x(g, j)
            if not (static(g) and g == 0):
                finish(g - 1)

        def finish(g):
            for j in range(GB):
                at_least(sp, ff.st_o[j], g * DMA + DMA, apart=True)
                sp.dma_start(res[j][:, :], x2_dram[g * GB + j]).then_inc(ff.ld_r[j], DMA)
            for j in range(GB):
                at_least(sp, ff.dv_o, g * GB + (j + 1), apart=True)
                sp.dma_start(out[g * GB + j], res[j][:, :]).then_inc(ff.st_o[j], DMA)

        def after():
            finish(NGRP - 1)
            for j in range(GB):
                sp.wait_ge(ff.st_o[j], (NGRP + 1) * DMA)

        run(sp, group, before, after)

    @block.tensor
    def _(pe):
        def gate(g):
            at_least(pe, ff.ac_m, g * GB - 1)
            for k in range(KT):
                pe.matmul(ff.BG[0:2 * NE, :], ff.ga[:, k, :, :].rearrange("p x n -> p (x n)"), ff.xT_hi[:, k, :],
                          start=k == 0, stop=False)
            for k in range(KT):
                mm = pe.matmul(ff.BG[0:NE, :], ff.ga_hi[:, k, :], ff.xT_lo[:, k, :], start=False, stop=k == KT - 1)
            mm.then_inc(ff.pe_G, 1)

        def downward(g, i):
            if static(g) and g == 0:
                pe.wait_ge(ff.fl, ff.have("down", i))
            at_least(pe, ff.dv_l, g * NI + (i + 1))
            for j in range(GB):
                c = slice(j * P, (j + 1) * P)
                if i == 0:
                    at_least(pe, ff.dv_y, (g - 1) * GB + (j + 1))
                mm = mm3(pe, bank[j], [(ff.hT_hi[i % 2][:, c], ff.hT_lo[i % 2][:, c])],
                         [ff.down[i]], first=i == 0, last=i == NI - 1)
            mm.then_inc(ff.pe_D, 1)

        def expert(g, j):
            if static(g) and g == 0 and j == 0:
                pe.wait_ge(ff.fl, ff.have("ex", KT - 1))
            c = slice(j * P, (j + 1) * P)
            if j == 0:
                at_least(pe, ff.ac_G, g + 1)
            elif j == 1:
                at_least(pe, ff.ac_r, g * NI + NI)
            else:
                at_least(pe, ff.ac_m, g * GB + (j - 1))
            mm3(pe, ff.BE[j], [(ff.xT_hi[:, k, c], ff.xT_lo[:, k, c]) for k in range(KT)],
                [(ff.ex_hi[:, k, :], ff.ex_lo[:, k, :]) for k in range(KT)]).then_inc(ff.pe_E, 1)

        def group(g):
            last = static(g) and g == NGRP - 1
            first = static(g) and g == 0
            if not first:
                ff.upward(pe, g, 0)
                gate(g)
            for i in range(1, NI):
                ff.upward(pe, g, i)
                if i == 1:
                    if first:
                        pe.wait_ge(dv_x2, NB)
                        pe.wait_ge(ff.fcst, 3)
                        gate(g)
                    at_least(pe, ff.ac_G, g + 1, apart=True)
                    for j in range(GB):
                        mm = pe.matmul(ff.BTG[:, j * NE:(j + 1) * NE], ff.lg[:, j * P:(j + 1) * P], ff.two_ident[:, :],
                                       start=True, stop=True)
                    mm.then_inc(ff.pe_TG, 1)
                downward(g, i - 1)
            for j in range(GB):
                expert(g, j)
                if not last:
                    ff.turn(pe, g + 1, j)
                elif j == 0:
                    downward(g, NI - 1)
            if not last:
                downward(g, NI - 1)

        run(pe, group)

    @block.scalar
    def _(act):
        def copy(dst, src):
            return act.activation(dst, src, ACT.Copy)

        def before():
            act.wait_ge(ff.ld_g, 4 * DMA)
            copy(ff.ga_hi, ff.ga_raw[:, :, :]).then_inc(ff.ga_split, 1)
            for n in range(1, ff.nstage):
                ff.piece_hi(act, n)

        def tile_hi(g, i):
            at_least(act, ff.pe_U, g * NI + (i + 1))
            at_least(act, ff.dv_h, g * NI + i)
            act.activation(ff.relu[:, :], bank[4 + i % 2], ACT.Relu).then_inc(ff.ac_r, 1)
            at_least(act, ff.dv_h, g * NI + (i + 1))
            at_least(act, ff.pe_D, g * NI + (i - 1))
            copy(ff.hT_hi[i % 2][:, :], ff.hid[:, :]).then_inc(ff.ac_h, 1)

        def weigh(g, j):
            at_least(act, ff.dv_s, g + 1)
            if static(g) and g == 0 and j == 0:
                act.wait_ge(ff.fl, len(ff.pieces))
            at_least(act, ff.pe_E, g * GB + (j + 1))
            at_least(act, ff.dv_o, (g - 1) * GB + (j + 1))
            act.activation(ff.y[j][:, :], ff.BE[j], ACT.Copy, scale=route[:, j:j + 1]).then_inc(ff.ac_m, 1)

        def group(g):
            last = static(g) and g == NGRP - 1
            for i in range(NI):
                tile_hi(g, i)
                if i == 0:
                    at_least(act, ff.pe_G, g + 1)
                    copy(ff.lg[:, :], ff.BG[0:2 * NE, :]).then_inc(ff.ac_G, 1)
                if static(g) and g == 0:
                    for n in due(i):
                        freed(act) if n == first_new else None
                        ff.piece_hi(act, n)
            for j in range(GB):
                weigh(g, j)
                if not last:
                    ff.hi_T(act, g + 1, j)

        run(act, group, before)

    @block.vector
    def _(dve):
        def hidden(g, i):
            at_least(dve, ff.ac_h, g * NI + i)
            at_least(dve, ff.dv_l, g * NI + i)
            at_least(dve, ff.ac_r, g * NI + (i + 1))
            dve.tensor_tensor(ff.hid[:, :], ff.relu[:, :], ff.relu[:, :], ALU.mult).then_inc(ff.dv_h, 1)
            at_least(dve, ff.ac_h, g * NI + (i + 1))
            dve.tensor_tensor(ff.hT_lo[i % 2][:, :], ff.hid[:, :], ff.hT_hi[i % 2][:, :].bitcast(F32), ALU.subtract).then_inc(ff.dv_l, 1)

        def routing(g):
            at_least(dve, ff.pe_TG, g + 1)
            at_least(dve, ff.ac_m, g * GB, apart=True)
            for j in range(GB):
                i = dve.max(top[:, j, :], ff.BTG[:, j * NE:(j + 1) * NE])
            i.then_inc(ff.dv_top, 1)
            at_least(dve, ff.dv_top, g + 1)
            dve.tensor_tensor(route[:, :], top[:, :, 0], top[:, :, 1], ALU.add).then_inc(ff.dv_s, 1)

        def add(g, j):
            at_least(dve, ff.pe_D, g * NI + NI)
            at_least(dve, ff.ac_m, g * GB + (j + 1))
            dve.tensor_tensor(ff.y[j][:, :], bank[j], ff.y[j][:, :], ALU.add).then_inc(ff.dv_y, 1)

        def y_stats(g, j):
            at_least(dve, ff.dv_y, g * GB + (j + 1))
            dve.bn_stats(yst6[:, j, :], ff.y[j][:, :]).then_inc(ff.dv_yb, 1)
            at_least(dve, ff.dv_yb, g * GB + (j + 1), apart=True)
            dve.bn_aggr(ymv[:, j, :], yst6[:, j, :]).then_inc(ff.dv_ys, 1)

        def result(g, j):
            at_least(dve, ff.dv_ys, g * GB + (j + 1))
            dve.scalar_tensor_tensor(out=ff.y[j][:, :], in0=ff.y[j][:, :], scalar=ymv[:, j, 0:1], in1=ff.gamma[:, :],
                                     op0=ALU.subtract, op1=ALU.mult).then_inc(ff.dv_a, 1)
            at_least(dve, ff.dv_a, g * GB + (j + 1))
            at_least(dve, ff.po_ys, g * GB + (j + 1))
            at_least(dve, ff.po_r, g * GB + (j + 1))
            dve.scalar_tensor_tensor(out=res[j][:, :], in0=ff.y[j][:, :], scalar=yrstd[:, j:j + 1], in1=res[j][:, :],
                                     op0=ALU.mult, op1=ALU.add).then_inc(ff.dv_o, 1)

        def group(g):
            last = static(g) and g == NGRP - 1
            for i in range(NI):
                hidden(g, i)
                if static(g) and g == 0:
                    for n in due(i):
                        freed(dve) if n == first_new else None
                        ff.piece_lo(dve, n)
                if i == 0:
                    routing(g)
                if not (static(g) and g == 0):
                    if 1 <= i <= GB:
                        y_stats(g - 1, i - 1)
                    if 2 <= i <= GB + 1:
                        result(g - 1, i - 2)
                if not last and i >= NI - 2 * GB:
                    (ff.normalise if i % 2 else ff.stats)(dve, g + 1, (i - (NI - 2 * GB)) // 2)
            if not last:
                for j in range(GB):
                    ff.lo_T(dve, g + 1, j)
            for j in range(GB):
                add(g, j)
                if last:
                    y_stats(g, j)
                    result(g, j)

        run(dve, group)

    @block.gpsimd
    def _(pool):
        def scale_y(g, j):
            at_least(pool, ff.dv_ys, g * GB + (j + 1), apart=True)
            pool.tensor_scalar(yvar[:, j:j + 1], ymv[:, j, 1:2], EPS_LN, None, ALU.add).then_inc(ff.po_yv, 1)
            at_least(pool, ff.po_yv, g * GB + (j + 1))
            pool.tensor_tensor(yrstd[:, j:j + 1], yvar[:, j:j + 1], powers[:, 0:1], ALU.pow).then_inc(ff.po_ys, 1)

        def residual(g, j):
            at_least(pool, ff.ld_r[j], g * DMA + DMA)
            pool.tensor_tensor(res[j][:, :], res[j][:, :], ff.beta[:, :], ALU.add).then_inc(ff.po_r, 1)

        def before():
            freed(pool)
            pool.wait_ge(ff.fcst, 3)

        def group(g):
            last = static(g) and g == NGRP - 1
            if not (static(g) and g == 0):
                finish(g - 1)
            if not last:
                for j in range(GB):
                    ff.inv_std(pool, g + 1, j)

        def finish(g):
            for j in range(GB):
                residual(g, j)
                scale_y(g, j)

        def after():
            finish(NGRP - 1)

        run(pool, group, before, after)


def kernel(**inputs):
    import numpy as np
    import concourse.bacc as bacc
    from concourse.bass_utils import run_bass_kernel_spmd

    def f(name):
        return np.asarray(inputs[name])

    def rows_on_partitions(w):
        return np.ascontiguousarray(w.reshape(-1, P, w.shape[1]).transpose(1, 0, 2).reshape(P, -1))

    ctxt = f("ctx_2048")
    nb = ctxt.shape[0]
    up = f("L0_ffn_up_w")
    arrays = {
        "x": f("x"),
        "ctxT": ctxt.transpose(0, 2, 1).reshape(nb, KT, P, P).transpose(0, 2, 1, 3).reshape(nb, P, KT * P),
        "ident": np.eye(P, dtype=np.float32),
        "two_ident": np.tile(np.eye(f("L0_ffn_gate_w").shape[1], dtype=np.float32), (2, 1)),
        "g_xattn": f("g_xattn").reshape(1, 1),
        "g_ffn": f("g_ffn").reshape(1, 1),
        "wq": rows_on_partitions(f("L0_xattn_q_w").T),
        "wk": rows_on_partitions(f("L0_xattn_k_img_w").T),
        "wv": rows_on_partitions(f("L0_xattn_v_img_w").T),
        "wo": rows_on_partitions(f("L0_xattn_o_w").T),
        "bq": f("L0_xattn_q_b").reshape(1, D),
        "bk": f("L0_xattn_k_img_b").reshape(1, D),
        "bv": f("L0_xattn_v_img_b").reshape(1, D),
        "bo": f("L0_xattn_o_b").reshape(1, D),
        "nq": f("L0_xattn_norm_q_w").reshape(1, D),
        "nk": f("L0_xattn_norm_k_img_w").reshape(1, D),
        "gate": rows_on_partitions(f("L0_ffn_gate_w")),
        "up": up.reshape(KT, P, -1, P).transpose(1, 2, 0, 3).reshape(P, -1),
        "down": rows_on_partitions(f("L0_ffn_down_w")),
        "ex": rows_on_partitions(f("L0_ffn_expert_weight")),
        "gamma": f("L0_ffn_ln_gamma").reshape(1, D),
        "beta": f("L0_ffn_ln_beta").reshape(1, D),
    }
    arrays = {n: np.ascontiguousarray(a) for n, a in arrays.items()}
    nc = bacc.Bacc("TRN2", target_bir_lowering=False, num_devices=1)
    t = {n: nc.dram_tensor("in_" + n, a.shape, mybir.dt.from_np(a.dtype), kind="ExternalInput").ap() for n, a in arrays.items()}
    out = nc.dram_tensor("out_x", arrays["x"].shape, F32, kind="ExternalOutput").ap()
    flamingo_layer(nc, t, out)
    r = run_bass_kernel_spmd(nc, [{"in_" + n: a for n, a in arrays.items()}], core_ids=[0])
    return r.results[0]["out_x"]
```
